# Optimizing a Trainium2 kernel written in Bass

```python
import numpy as np
import jax
import jax.numpy as jnp

def _softmax(x, axis=-1):
    return jax.nn.softmax(x, axis=axis)

def _gelu(x):
    return jax.nn.gelu(x, approximate=True)

def _silu(x):
    return jax.nn.silu(x)

def _sigmoid(x):
    return jax.nn.sigmoid(x)

def _layernorm(x, axis=-1, eps=1e-05):
    m = jnp.mean(x, axis=axis, keepdims=True)
    v = jnp.var(x, axis=axis, keepdims=True)
    return (x - m) / jnp.sqrt(v + eps)

def _scatter_add(tgt, idx, src, axis=0):
    return tgt.at[idx].add(src)

def _segment_sum(src, seg, n):
    return jax.ops.segment_sum(src, seg, n)
kernel_name = 'mk_seq_preln_d1_jaxref_r4_335a24'

def setup_inputs(seed: int=0):
    np.random.seed(seed)
    _w = jnp.asarray

    def _L0_attn_setup():
        import jax, jax.numpy as jnp
        from jax import lax
        import numpy as np
        D_MODEL, D_STATE, D_CONV, EXPAND = (256, 16, 4, 2)
        D_INNER = EXPAND * D_MODEL
        DT_RANK = D_MODEL // 16
        B_SZ, L_SEQ = (2, 512)

        def _selective_scan(u, dt, A, Bm, Cm, Dvec):

            def step(h, inputs):
                u_t, dt_t, B_t, C_t = inputs
                dA = jnp.exp(dt_t[:, :, None] * A[None])
                dBu = (dt_t * u_t)[:, :, None] * B_t[:, None, :]
                h = dA * h + dBu
                y = jnp.einsum('bdn,bn->bd', h, C_t)
                return (h, y)
            xs = (u.transpose(1, 0, 2), dt.transpose(1, 0, 2), Bm.transpose(1, 0, 2), Cm.transpose(1, 0, 2))
            h0 = jnp.zeros((u.shape[0], u.shape[2], A.shape[1]), u.dtype)
            _, ys = lax.scan(step, h0, xs)
            return ys.transpose(1, 0, 2) + u * Dvec
        key = jax.random.key(seed)
        ks = jax.random.split(key, 8)
        x = jax.random.normal(ks[0], (B_SZ, L_SEQ, D_MODEL), jnp.float32)
        inp = {'x': x, 'ln_g': jnp.ones((D_MODEL,), jnp.float32), 'ln_b': jnp.zeros((D_MODEL,), jnp.float32), 'W_in': jax.random.normal(ks[1], (2 * D_INNER, D_MODEL), jnp.float32) / np.sqrt(D_MODEL), 'conv_w': jax.random.normal(ks[2], (D_INNER, D_CONV), jnp.float32) / np.sqrt(D_CONV), 'conv_b': jnp.zeros((D_INNER,), jnp.float32), 'W_xp': jax.random.normal(ks[3], (DT_RANK + 2 * D_STATE, D_INNER), jnp.float32) / np.sqrt(D_INNER), 'W_dt': jax.random.normal(ks[4], (D_INNER, DT_RANK), jnp.float32) / np.sqrt(DT_RANK), 'b_dt': jax.random.normal(ks[5], (D_INNER,), jnp.float32) * 0.1 - 4.0, 'A_log': jnp.broadcast_to(jnp.log(jnp.arange(1, D_STATE + 1, dtype=jnp.float32)), (D_INNER, D_STATE)).copy(), 'D': jnp.ones((D_INNER,), jnp.float32), 'W_out': jax.random.normal(ks[6], (D_MODEL, D_INNER), jnp.float32) / np.sqrt(D_INNER)}
        return inp
    _L0_attn_in = _L0_attn_setup()

    def _L0_ffn_setup():
        import jax, jax.numpy as jnp
        import numpy as np
        EMBED = 256
        NUM_EXPERTS = 8
        TOP_K = 2
        key = jax.random.key(seed)
        ks = jax.random.split(key, 6)
        scale = EMBED ** (-0.5)
        return {'x': jax.random.normal(ks[0], (4, 1024, EMBED), jnp.float32), 'router_w': jax.random.normal(ks[1], (EMBED, NUM_EXPERTS), jnp.float32) * scale, 'router_b': jnp.zeros((NUM_EXPERTS,), jnp.float32), 'we_gate': jax.random.normal(ks[2], (NUM_EXPERTS, EMBED, EMBED), jnp.float32) * scale, 'we_up': jax.random.normal(ks[3], (NUM_EXPERTS, EMBED, EMBED), jnp.float32) * scale, 'we_down': jax.random.normal(ks[4], (NUM_EXPERTS, EMBED, EMBED), jnp.float32) * scale}
    _L0_ffn_in = _L0_ffn_setup()
    _d = {'L0_attn_x': _L0_attn_in['x'], 'L0_attn_ln_g': _L0_attn_in['ln_g'], 'L0_attn_ln_b': _L0_attn_in['ln_b'], 'L0_attn_W_in': _L0_attn_in['W_in'], 'L0_attn_conv_w': _L0_attn_in['conv_w'], 'L0_attn_conv_b': _L0_attn_in['conv_b'], 'L0_attn_W_xp': _L0_attn_in['W_xp'], 'L0_attn_W_dt': _L0_attn_in['W_dt'], 'L0_attn_b_dt': _L0_attn_in['b_dt'], 'L0_attn_A_log': _L0_attn_in['A_log'], 'L0_attn_D': _L0_attn_in['D'], 'L0_attn_W_out': _L0_attn_in['W_out'], 'L0_ffn_router_w': _L0_ffn_in['router_w'], 'L0_ffn_router_b': _L0_ffn_in['router_b'], 'L0_ffn_we_gate': _L0_ffn_in['we_gate'], 'L0_ffn_we_up': _L0_ffn_in['we_up'], 'L0_ffn_we_down': _L0_ffn_in['we_down']}
    _x0 = _d['L0_attn_x']
    _d['L0_attn_x'] = jax.random.normal(jax.random.fold_in(jax.random.key(seed), 1), (8, 1024, 256), dtype=_x0.dtype)
    del _x0
    return _d

def reference(L0_attn_x, L0_attn_ln_g, L0_attn_ln_b, L0_attn_W_in, L0_attn_conv_w, L0_attn_conv_b, L0_attn_W_xp, L0_attn_W_dt, L0_attn_b_dt, L0_attn_A_log, L0_attn_D, L0_attn_W_out, L0_ffn_router_w, L0_ffn_router_b, L0_ffn_we_gate, L0_ffn_we_up, L0_ffn_we_down):

    def _L0_attn_ref(x, ln_g, ln_b, W_in, conv_w, conv_b, W_xp, W_dt, b_dt, A_log, D, W_out):
        import jax, jax.numpy as jnp
        from jax import lax
        import numpy as np
        D_MODEL, D_STATE, D_CONV, EXPAND = (256, 16, 4, 2)
        D_INNER = EXPAND * D_MODEL
        DT_RANK = D_MODEL // 16
        B_SZ, L_SEQ = (2, 512)

        def _selective_scan(u, dt, A, Bm, Cm, Dvec):

            def step(h, inputs):
                u_t, dt_t, B_t, C_t = inputs
                dA = jnp.exp(dt_t[:, :, None] * A[None])
                dBu = (dt_t * u_t)[:, :, None] * B_t[:, None, :]
                h = dA * h + dBu
                y = jnp.einsum('bdn,bn->bd', h, C_t)
                return (h, y)
            xs = (u.transpose(1, 0, 2), dt.transpose(1, 0, 2), Bm.transpose(1, 0, 2), Cm.transpose(1, 0, 2))
            h0 = jnp.zeros((u.shape[0], u.shape[2], A.shape[1]), u.dtype)
            _, ys = lax.scan(step, h0, xs)
            return ys.transpose(1, 0, 2) + u * Dvec
        d_inner, d_conv = conv_w.shape
        dt_rank = W_dt.shape[1]
        d_state = A_log.shape[1]
        mu = jnp.mean(x, axis=-1, keepdims=True)
        var = jnp.mean(jnp.square(x - mu), axis=-1, keepdims=True)
        xn = (x - mu) * lax.rsqrt(var + 1e-05) * ln_g + ln_b
        xz = jnp.einsum('bld,ed->ble', xn, W_in)
        u, z = jnp.split(xz, 2, axis=-1)
        u_c = lax.conv_general_dilated(u.transpose(0, 2, 1), conv_w[:, None, :], window_strides=(1,), padding=[(d_conv - 1, 0)], feature_group_count=d_inner)
        u_c = jax.nn.silu((u_c + conv_b[None, :, None]).transpose(0, 2, 1))
        x_dbl = jnp.einsum('bld,ed->ble', u_c, W_xp)
        dt, Bm, Cm = jnp.split(x_dbl, [dt_rank, dt_rank + d_state], axis=-1)
        dt = jax.nn.softplus(jnp.einsum('blr,dr->bld', dt, W_dt) + b_dt)
        A = -jnp.exp(A_log)
        y = _selective_scan(u_c, dt, A, Bm, Cm, D)
        y = y * jax.nn.silu(z)
        out = jnp.einsum('ble,de->bld', y, W_out)
        return x + out

    def _L0_ffn_ref(x, router_w, router_b, we_gate, we_up, we_down):
        import jax, jax.numpy as jnp
        import numpy as np
        EMBED = 256
        NUM_EXPERTS = 8
        TOP_K = 2
        x_shape = x.shape
        x_flat = x.reshape(-1, x_shape[-1])
        num_tokens = x_flat.shape[0]
        router_logits = x_flat @ router_w + router_b
        topk_weights, topk_indices = jax.lax.top_k(router_logits, k=TOP_K)
        topk_weights = jax.nn.softmax(topk_weights, axis=-1)
        token_idx_mesh = jnp.repeat(jnp.arange(num_tokens), TOP_K)
        expert_idx_mesh = topk_indices.reshape(-1)
        sort_permutation = jnp.argsort(expert_idx_mesh)
        sorted_expert_idx = expert_idx_mesh[sort_permutation]
        sorted_token_idx = token_idx_mesh[sort_permutation]
        group_sizes = jnp.bincount(sorted_expert_idx, length=NUM_EXPERTS)
        sorted_tokens = x_flat[sorted_token_idx]
        ff_gate = jax.lax.ragged_dot(sorted_tokens, we_gate, group_sizes)
        ff_up = jax.lax.ragged_dot(sorted_tokens, we_up, group_sizes)
        activated = jax.nn.silu(ff_gate) * ff_up
        ff_out = jax.lax.ragged_dot(activated, we_down, group_sizes)
        sorted_weights = topk_weights.reshape(-1)[sort_permutation]
        ff_out = ff_out * sorted_weights[:, None]
        output_flat = jnp.zeros_like(x_flat).at[sorted_token_idx].add(ff_out)
        return output_flat.reshape(x_shape)
    x = L0_attn_x
    x = x + _L0_attn_ref(_layernorm(x, axis=-1), L0_attn_ln_g, L0_attn_ln_b, L0_attn_W_in, L0_attn_conv_w, L0_attn_conv_b, L0_attn_W_xp, L0_attn_W_dt, L0_attn_b_dt, L0_attn_A_log, L0_attn_D, L0_attn_W_out)
    x = x + _L0_ffn_ref(_layernorm(x, axis=-1), L0_ffn_router_w, L0_ffn_router_b, L0_ffn_we_gate, L0_ffn_we_up, L0_ffn_we_down)
    return x

_drawn_inputs = setup_inputs


def setup_inputs(seed=0):
    import zlib

    import numpy as np

    out = dict(_drawn_inputs(seed))
    spreads = {'L0_attn_ln_g': (1.0, 0.2),
     'L0_attn_ln_b': (0.0, 0.1),
     'L0_attn_conv_b': (0.0, 0.1),
     'L0_attn_D': (1.0, 0.6),
     'L0_ffn_router_b': (0.0, 0.8)}
    factors = {'L0_attn_b_dt': 64.0,
     'L0_attn_W_xp': 8.0,
     'L0_attn_W_dt': 8.0,
     'L0_attn_A_log': 2.717,
     'L0_ffn_router_w': 8.0,
     'L0_ffn_we_gate': 8.0,
     'L0_ffn_we_up': 8.0,
     'L0_ffn_we_down': 8.0}
    for name, (base, spread) in spreads.items():
        noise = np.random.default_rng([zlib.crc32(name.encode()), seed]).standard_normal(out[name].shape)
        drawn = base * np.exp(spread * noise) if base else spread * noise
        out[name] = jnp.asarray(drawn.astype(out[name].dtype))
    for name, factor in factors.items():
        out[name] = (out[name] * factor).astype(out[name].dtype)
    return out
```

```python
from contextlib import ExitStack

import numpy as np

import concourse.bass as bass
from concourse import mybir

F32 = mybir.dt.float32
U32 = mybir.dt.uint32
ALU = mybir.AluOpType
ACT = mybir.ActivationFunctionType

P = 128
BATCH, SEQ, DM = 8, 1024, 256
DI, NS, TAPS, RANK = 512, 16, 4, 16
NE = 8
T = 512
NQ = BATCH * SEQ // T
NT = T // P
DC = DM // P
CC = DI // P
R = 4
G = NS // R
J = P // 32
UN = CC * G
EPS = 1e-5

FT_X, FT_Z, FT_U, FT_XD, FT_DT = 0, DC, DC + CC, DC + 2 * CC, DC + 2 * CC + 1
FT = FT_DT + CC
TP_O, TP_A, TP_B, TP_E = 0, 1, 2, 3
EXPERT_PIECES = []
for _e in range(NE):
    EXPERT_PIECES += [("gu", _e, 0), ("gu", _e, 1)]
    if _e:
        EXPERT_PIECES.append(("down", _e - 1, 0))
EXPERT_PIECES.append(("down", NE - 1, 0))
TP = TP_E + len(EXPERT_PIECES)
RELEASE = []
for _k in range(TP):
    _who = "act" if _k == TP_A or (_k >= TP_E and EXPERT_PIECES[_k - TP_E][0] == "down") else "dve"
    RELEASE.append((_who, sum(r[0] == _who for r in RELEASE) + 1))
REL_N = {w: sum(r[0] == w for r in RELEASE) for w in ("act", "dve")}
PAIR_AT = {p: TP_E + k for k, p in enumerate(EXPERT_PIECES)}
FIRST, LAST = 5, 15


def mamba_moe(nc, x, w_in, w_xp, w_dt, w_out, w_moe, chan, a_log, ln_gb, r_w, r_b, consts, out):
    with ExitStack() as ctx:
        def sb(name, shape, dt=F32):
            return ctx.enter_context(nc.sbuf_tensor(name, shape, dt))

        def sem(name):
            return ctx.enter_context(nc.semaphore(name))

        w_in_s = sb("w_in_s", [P, DC, 2 * DI])
        w_xp_s = sb("w_xp_s", [P, CC, RANK + 2 * NS])
        w_dt_s = sb("w_dt_s", [P, DI])
        w_out_s = sb("w_out_s", [P, CC, DM])
        chan_s = sb("chan_s", [P, CC, TAPS + 3])
        a_s = sb("a_s", [P, UN, J])
        ln_s = sb("ln_s", [P, 2, DC])
        rw_s = sb("rw_s", [P, DC, NE])
        rb_s = sb("rb_s", [P, NE])
        const_s = sb("const_s", [P, P + 32 + NE])
        ident = const_s[:, 0:P]
        sumsel = const_s[:, P:P + 32]
        iota = const_s[:, P + 32:P + 32 + NE]
        nhalf = sb("nhalf", [P, NT])
        eps = sb("eps", [P, NT])
        w_e = sb("w_e", [P, 2, DC * 2 * DM + 2 * DM])

        xin = sb("xin", [P, NT, DM])
        xs = sb("xs", [P, 2, NT, DM])
        xn = sb("xn", [P, NT, DM])
        xnT = sb("xnT", [P, DC, T])
        stats = sb("stats", [P, 2, NT, 6])
        mv = sb("mv", [P, 2, NT, 2])
        rst = sb("rst", [P, 2, NT, 4])
        ubuf = sb("ubuf", [P, 2, T + TAPS - 1])
        halo = sb("halo", [P, CC, TAPS - 1])
        uc = sb("uc", [P, 2, CC, T])
        sz = sb("sz", [P, 2, CC, T])
        xd = sb("xd", [P, T])
        t_e = sb("t_e", [P, T])
        t_r = sb("t_r", [P, T])
        t_m = sb("t_m", [P, T])
        dtb = sb("dtb", [P, 2, T])
        dtub = sb("dtub", [P, 2, T])

        b_bc = sb("b_bc", [P, G, T])
        c_bc = sb("c_bc", [P, G, T])
        rep_dt = sb("rep_dt", [P, 2, J, T])
        rep_dtu = sb("rep_dtu", [P, 2, J, T])
        dA = sb("dA", [P, 2, J, T])
        dBu = sb("dBu", [P, 2, J, T])
        carry = sb("carry", [P, UN, J])

        x2 = sb("x2", [P, NT, DM])
        xf = sb("xf", [P, NT, DM])
        xfT = sb("xfT", [P, DC, T])
        lg = sb("lg", [P, NT, NE])
        mx = sb("mx", [P, NT, 8])
        ix = sb("ix", [P, NT, 8], U32)
        ixf = sb("ixf", [P, NT, 2])
        gap = sb("gap", [P, NT, 4])
        wts = sb("wts", [P, 2, NT, NE])
        th = sb("th", [P, 2, T])
        hT = sb("hT", [P, 2, 2, T])

        fr = ctx.enter_context(nc.psum_tensor("fr", [P, 2, 512], F32))
        mo = ctx.enter_context(nc.psum_tensor("mo", [P, 2, 2, 512], F32))
        yps = ctx.enter_context(nc.psum_tensor("yps", [P, 2, 512], F32))

        bc_d = nc.dram_tensor("bc_d", (2 * NS, T), F32, kind="Internal").ap()
        dt_d = nc.dram_tensor("dt_d", (2, 2, CC, P, T), F32, kind="Internal").ap()

        s_w = sem("s_w")
        s_init = sem("s_init")
        s_a = sem("s_a")
        s_x = sem("s_x")
        s_xs = sem("s_xs")
        s_bn = sem("s_bn")
        s_agg = sem("s_agg")
        s_mv = sem("s_mv")
        s_rs = sem("s_rs")
        s_pow = sem("s_pow")
        s_y = sem("s_y")
        s_xn = sem("s_xn")
        s_fr = sem("s_fr")
        s_fra = sem("s_fra")
        s_frd = sem("s_frd")
        s_xnT = sem("s_xnT")
        s_u = sem("s_u")
        s_tap = sem("s_tap")
        s_conv = sem("s_conv")
        s_uc = sem("s_uc")
        s_z = sem("s_z")
        s_sz = sem("s_sz")
        s_xd = sem("s_xd")
        s_bcw = sem("s_bcw")
        s_abs = sem("s_abs")
        s_e = sem("s_e")
        s_l = sem("s_l")
        s_m = sem("s_m")
        s_sp = sem("s_sp")
        s_dt = sem("s_dt")
        s_dtw = [sem(f"s_dtw{i}") for i in range(2)]
        s_bc = [sem(f"s_bc{g}") for g in range(G)]
        s_rdt = [sem(f"s_rdt{i}") for i in range(2)]
        s_rdtu = [sem(f"s_rdtu{i}") for i in range(2)]
        s_exp = sem("s_exp")
        s_dbu = sem("s_dbu")
        s_scan = sem("s_scan")
        s_carry = sem("s_carry")
        s_hc = sem("s_hc")
        s_ymm = sem("s_ymm")
        s_yd = sem("s_yd")
        s_yg = sem("s_yg")
        s_mo = sem("s_mo")
        s_moa = sem("s_moa")
        s_mod = sem("s_mod")
        s_x2 = sem("s_x2")
        s_mv2 = sem("s_mv2")
        s_pow2 = sem("s_pow2")
        s_rs2 = sem("s_rs2")
        s_xf = sem("s_xf")
        s_xfT = sem("s_xfT")
        s_lg = sem("s_lg")
        s_gap = sem("s_gap")
        s_ge = sem("s_ge")
        s_wts = sem("s_wts")
        s_th = sem("s_th")
        s_ga = sem("s_ga")
        s_h = sem("s_h")
        s_sc = sem("s_sc")
        s_acc = sem("s_acc")
        s_wgu = [sem(f"s_wgu{i}") for i in range(2)]
        s_wdn = [sem(f"s_wdn{i}") for i in range(2)]
        s_out = sem("s_out")
        LG = 9

        x_v = x.rearrange("b (h i p) d -> (b h) p i d", h=SEQ // T, p=P)
        out_v = out.rearrange("b (h i p) d -> (b h) p i d", h=SEQ // T, p=P)

        def chunk(v, q):
            return v[q] if isinstance(q, int) else v[bass.ds(q, 1)].rearrange("a p i d -> p (a i) d")

        def wait(eng, s, value):
            if isinstance(value, int) and value <= 0:
                return
            eng.wait_ge(s, value)

        def counts(eng, *values):
            return [v if isinstance(v, int) else eng.snap(eng.to_reg(v), min_val=0, max_val=1 << 15) for v in values]

        def steps(eng, step):
            step(0, 0, True, False)
            step(1, 1, True, True)
            with eng.Fori(0, (NQ - 4) // 2) as i:
                step(i * 2 + 2, 0, True, True)
                step(i * 2 + 3, 1, True, True)
            step(NQ - 2, 0, True, True)
            step(NQ - 1, 1, False, True)
            step(NQ, 0, None, True)

        def pieces(n):
            if not FIRST <= n < LAST:
                return range(0)
            k = len(EXPERT_PIECES)
            return range(k * (n - FIRST) // (LAST - FIRST), k * (n - FIRST + 1) // (LAST - FIRST))

        block = ctx.enter_context(nc.Block())

        @block.sync
        def _(sp):
            for dst, src in ((w_in_s, w_in), (w_xp_s, w_xp), (w_dt_s, w_dt), (w_out_s, w_out), (chan_s, chan),
                             (a_s, a_log), (ln_s, ln_gb), (rw_s, r_w), (rb_s, r_b), (const_s, consts)):
                sp.dma_start(dst[:], src).then_inc(s_w, 16)

            def number(q):
                return q if isinstance(q, int) else sp.snap(q, min_val=0, max_val=NQ - 1)

            def load_x(q):
                at = number(q)
                wait(sp, s_xs, q)
                sp.dma_start(xin[:], chunk(x_v, at)).then_inc(s_x, 16)

            def store_bc(q):
                wait(sp, s_xd, q + 1)
                sp.dma_start(bc_d, xd[RANK:RANK + 2 * NS, :]).then_inc(s_bcw, 16)

            def load_bc(q, g):
                stored, used = counts(sp, 16 * q + 16, UN * q - G + g + 1)
                wait(sp, s_bcw, stored)
                wait(sp, s_dbu, used)
                wait(sp, s_hc, used)
                for dst, row in ((b_bc, 0), (c_bc, NS)):
                    for r in range(R):
                        src = bc_d[row + R * g + r:row + R * g + r + 1, :].to_broadcast([32, T])
                        sp.dma_start(dst[32 * r:32 * r + 32, g, :], src).then_inc(s_bc[g], 16)

            def store_dt(q, pq, c):
                wait(sp, s_dt, CC * q + c + 1)
                sp.dma_start(dt_d[pq, 0, c], dtb[:, c % 2, :]).then_inc(s_dtw[c % 2], 16)
                sp.dma_start(dt_d[pq, 1, c], dtub[:, c % 2, :]).then_inc(s_dtw[c % 2], 16)

            def load_rep(q, pq, c):
                stored, used = counts(sp, 32 * (2 * q + c // 2 + 1), G * (CC * q + c - 1))
                wait(sp, s_dtw[c % 2], stored)
                wait(sp, s_exp, used)
                wait(sp, s_dbu, used)
                for k, (dst, s) in enumerate(((rep_dt, s_rdt), (rep_dtu, s_rdtu))):
                    src = dt_d[pq, k, c].rearrange("(j d) t -> d j t", j=J)
                    for r in range(R):
                        sp.dma_start(dst[32 * r:32 * r + 32, c % 2], src).then_inc(s[c % 2], 16)

            def load_expert(q, e, kind):
                piece = ("gu", (e - 2) % NE, 1) if kind == "gu" else ("down", (e - 2) % NE, 0)
                wait(sp, s_mo, TP * (q if e >= 2 else q - 1) + PAIR_AT[piece] + 1)
                lo, hi = (0, DC * 2 * DM) if kind == "gu" else (DC * 2 * DM, DC * 3 * DM)
                sp.dma_start(w_e[:, e % 2, lo:hi], w_moe[e, :, lo:hi]).then_inc((s_wgu if kind == "gu" else s_wdn)[e % 2], 16)

            def step(q, pq, front, tail):
                scan = front is not None
                if scan:
                    load_rep(q, pq, 1)
                if front:
                    load_x(q + 1)
                for n in range(UN):
                    if scan and n == 4:
                        load_rep(q, pq, 2)
                    if scan and n == 8:
                        load_rep(q, pq, 3)
                    if front and n == 9:
                        store_bc(q + 1)
                    if front and n >= 11:
                        if n == 13:
                            load_rep(q + 1, 1 - pq, 0)
                        if n < 15:
                            store_dt(q + 1, 1 - pq, n - 11)
                    if front and n >= 13:
                        load_bc(q + 1, n - 13)
                    if tail:
                        for k in pieces(n):
                            kind, e, f = EXPERT_PIECES[k]
                            if e + 2 < NE and (kind, f) != ("gu", 0):
                                load_expert(q - 1, e + 2, kind)
                if front:
                    load_bc(q + 1, G - 1)
                if tail:
                    at = number(q - 1)
                    wait(sp, s_acc, NE * (q - 1) + NE)
                    sp.dma_start(chunk(out_v, at), x2[:]).then_inc(s_out, 16)
                if scan:
                    for e in range(2):
                        load_expert(q, e, "gu")
                        load_expert(q, e, "down")

            load_x(0)
            store_bc(0)
            for g in range(G):
                load_bc(0, g)
            for c in range(CC):
                store_dt(0, 0, c)
            load_rep(0, 0, 0)
            steps(sp, step)
            sp.wait_ge(s_out, 16 * NQ)

        @block.tensor
        def _(pe):
            pe.wait_ge(s_w, 160)
            pe.wait_ge(s_init, 2)

            def front_tile(q, pq, k):
                wait(pe, s_fra, FT * q + k - 1)
                j = (k - 2) % FT
                if j >= FT_DT:
                    wait(pe, s_frd, CC * (q if k >= 2 else q - 1) + j - FT_DT + 1)
                return fr[:, (FT * pq + k) % 2, :]

            def transpose_x(q, pq):
                for c in range(DC):
                    dst = front_tile(q, pq, FT_X + c)
                    wait(pe, s_xn, q + 1)
                    for i in range(NT):
                        last = pe.transpose(dst[:, i * P:(i + 1) * P], xn[:, i, c * P:(c + 1) * P], ident)
                    last.then_inc(s_fr, 1)

            def in_proj(q, pq, k, ch):
                dst = front_tile(q, pq, k)
                wait(pe, s_xnT, DC * (q + 1))
                for c in range(DC):
                    last = pe.matmul(dst, w_in_s[:, c, ch * P:(ch + 1) * P], xnT[:, c, :], start=c == 0, stop=c == DC - 1)
                last.then_inc(s_fr, 1)

            def x_proj(q, pq):
                dst = front_tile(q, pq, FT_XD)
                wait(pe, s_uc, CC * (q + 1))
                for c in range(CC):
                    last = pe.matmul(dst[0:RANK + 2 * NS, :], w_xp_s[:, c, :], uc[:, pq, c, :], start=c == 0, stop=c == CC - 1)
                last.then_inc(s_fr, 1)

            def dt_proj(q, pq, c):
                dst = front_tile(q, pq, FT_DT + c)
                wait(pe, s_xd, q + 1)
                pe.matmul(dst, w_dt_s[:, c * P:(c + 1) * P], xd[:], start=True, stop=True).then_inc(s_fr, 1)

            def unit(q, n):
                c, g = n // G, n % G
                if g == 0:
                    wait(pe, s_yg, CC * q + c - 1)
                wait(pe, s_hc, UN * q + n + 1)
                for j in range(J):
                    last = pe.matmul(yps[32 * j:32 * j + 32, c % 2, :], sumsel, dA[:, n % 2, j, :],
                                     start=g == 0, stop=g == G - 1)
                last.then_inc(s_ymm, 1)

            def tail_pair(q, pq, k):
                who, count = RELEASE[(k - 2) % TP]
                wait(pe, s_moa if who == "act" else s_mod, REL_N[who] * (q if k >= 2 else q - 1) + count)
                return mo[:, (TP * pq + k) % 2]

            def out_proj(q, pq):
                dst = tail_pair(q, pq, TP_O).rearrange("p a (b d) -> p (a b) d", d=DM)
                wait(pe, s_yg, CC * (q + 1))
                for i in range(NT):
                    for c in range(CC):
                        last = pe.matmul(dst[:, i, :], sz[:, pq, c, i * P:(i + 1) * P], w_out_s[:, c, :],
                                         start=c == 0, stop=c == CC - 1)
                last.then_inc(s_mo, 1)

            def transpose_xf(q, pq):
                dst = tail_pair(q, pq, TP_A)
                wait(pe, s_xf, q + 1)
                for c in range(DC):
                    for i in range(NT):
                        last = pe.transpose(dst[:, c, i * P:(i + 1) * P], xf[:, i, c * P:(c + 1) * P], ident)
                last.then_inc(s_mo, 1)

            def router(q, pq):
                dst = tail_pair(q, pq, TP_B)
                wait(pe, s_xfT, q + 1)
                for i in range(NT):
                    for c in range(DC):
                        last = pe.matmul(dst[:, 0, i * NE:(i + 1) * NE], xfT[:, c, i * P:(i + 1) * P], rw_s[:, c, :],
                                         start=c == 0, stop=c == DC - 1)
                last.then_inc(s_mo, 1)

            def expert(q, pq, k):
                kind, e, f = EXPERT_PIECES[k]
                dst = tail_pair(q, pq, TP_E + k)
                w = w_e[:, e % 2, :]
                if kind == "gu":
                    wait(pe, s_wgu[e % 2], 16 * ((NE // 2) * q + e // 2 + 1))
                    for a in range(2):
                        for c in range(DC):
                            col = c * 2 * DM + a * DM + f * P
                            last = pe.matmul(dst[:, a, :], w[:, col:col + P], xfT[:, c, :], start=c == 0, stop=c == DC - 1)
                else:
                    wait(pe, s_wdn[e % 2], 16 * ((NE // 2) * q + e // 2 + 1))
                    wait(pe, s_h, 2 * (NE * q + e + 1))
                    rows = dst.rearrange("p a (b d) -> p (a b) d", d=DM)
                    for i in range(NT):
                        for f in range(2):
                            col = 2 * DC * DM + f * DM
                            last = pe.matmul(rows[:, i, :], hT[:, e % 2, f, i * P:(i + 1) * P], w[:, col:col + DM],
                                             start=f == 0, stop=f == 1)
                last.then_inc(s_mo, 1)

            def front_slot(q, pq, n):
                if n == 2:
                    transpose_x(q, pq)
                if n == 3:
                    for c in range(CC):
                        in_proj(q, pq, FT_Z + c, CC + c)
                if n in (4, 5, 6, 7):
                    in_proj(q, pq, FT_U + n - 4, n - 4)
                if n == 9:
                    x_proj(q, pq)
                if n in (10, 11, 12, 13):
                    dt_proj(q, pq, n - 10)

            def step(q, pq, front, tail):
                scan = front is not None
                for n in range(UN):
                    if n and scan:
                        unit(q, n - 1)
                    if n == 0 and tail:
                        unit(q - 1, UN - 1)
                    if tail:
                        if n == 1:
                            out_proj(q - 1, 1 - pq)
                        if n == 4:
                            transpose_xf(q - 1, 1 - pq)
                        if n == 5:
                            router(q - 1, 1 - pq)
                    if front:
                        front_slot(q + 1, 1 - pq, n)
                    if tail:
                        for k in pieces(n):
                            expert(q - 1, 1 - pq, k)

            for n in range(UN):
                front_slot(0, 0, n)
            steps(pe, step)

        @block.scalar
        def _(act):
            act.wait_ge(s_w, 160)
            act.activation(a_s[:], a_s[:], ACT.Exp).then_inc(s_a, 1)
            act.wait_ge(s_a, 1)
            act.activation(a_s[:], a_s[:], ACT.Copy, scale=-1.0).then_inc(s_a, 1)
            act.wait_ge(s_a, 2)

            def take_x(q, pq):
                for c in range(DC):
                    wait(act, s_fr, FT * q + FT_X + c + 1)
                    act.activation(xnT[:, c, :], fr[:, (FT * pq + FT_X + c) % 2, :], ACT.Identity,
                                   scale=ln_s[:, 0, c:c + 1], bias=ln_s[:, 1, c:c + 1]).then_inc(s_xnT, 1)
                    act.wait_ge(s_xnT, DC * q + c + 1)
                    act.sem_inc(s_fra, 1)

            def take_u(q, pq, c):
                wait(act, s_fr, FT * q + FT_U + c + 1)
                wait(act, s_conv, CC * q + c - 1)
                act.activation(ubuf[:, c % 2, TAPS - 1:], fr[:, (FT * pq + FT_U + c) % 2, :], ACT.Copy).then_inc(s_u, 1)
                act.wait_ge(s_u, CC * q + c + 1)
                act.sem_inc(s_fra, 1)

            def take_z(q, pq):
                for c in range(CC):
                    wait(act, s_fr, FT * q + FT_Z + c + 1)
                    act.activation(sz[:, pq, c, :], fr[:, (FT * pq + FT_Z + c) % 2, :], ACT.Copy).then_inc(s_z, 1)
                    act.wait_ge(s_z, CC * q + c + 1)
                    act.sem_inc(s_fra, 1)

            def silus(q, pq):
                act.activation(sz[:, pq], sz[:, pq], ACT.Silu).then_inc(s_sz, 1)
                for c in range(CC):
                    wait(act, s_conv, CC * q + c + 1)
                    act.activation(uc[:, pq, c, :], uc[:, pq, c, :], ACT.Silu, bias=chan_s[:, c, TAPS:TAPS + 1]).then_inc(s_uc, 1)

            def take_xd(q, pq):
                wait(act, s_fr, FT * q + FT_XD + 1)
                wait(act, s_bcw, 16 * q)
                n = RANK + 2 * NS
                act.activation(xd[0:n, :], fr[0:n, (FT * pq + FT_XD) % 2, :], ACT.Copy).then_inc(s_xd, 1)
                act.wait_ge(s_xd, q + 1)
                act.sem_inc(s_fra, 1)

            def softplus(q, pq, c):
                v = CC * q + c
                wait(act, s_fr, FT * q + FT_DT + c + 1)
                wait(act, s_dt, v)
                act.activation(t_e[:], fr[:, (FT * pq + FT_DT + c) % 2, :], ACT.Abs,
                               bias=chan_s[:, c, TAPS + 1:TAPS + 2]).then_inc(s_abs, 1)
                act.wait_ge(s_abs, v + 1)
                act.sem_inc(s_fra, 1)
                act.activation(t_e[:], t_e[:], ACT.Exp, scale=-1.0).then_inc(s_e, 1)
                act.wait_ge(s_e, v + 1)
                wait(act, s_dtw[c % 2], 32 * (2 * q + c // 2))
                act.activation(dtb[:, c % 2, :], t_e[:], ACT.Ln, bias=1.0).then_inc(s_l, 1)

            def unit(q, n):
                c = n // G
                if n % G == 0:
                    wait(act, s_rdt[c % 2], 64 * (2 * q + c // 2 + 1))
                wait(act, s_ymm, UN * q + n - 1)
                for j in range(J):
                    last = act.activation(dA[:, n % 2, j, :], rep_dt[:, c % 2, j, :], ACT.Exp, scale=a_s[:, n, j:j + 1])
                last.then_inc(s_exp, 1)

            def take_xf(q, pq):
                wait(act, s_mo, TP * q + TP_A + 1)
                act.activation(xfT[:], mo[:, (TP * pq + TP_A) % 2], ACT.Copy).then_inc(s_xfT, 1)
                act.wait_ge(s_xfT, q + 1)
                act.sem_inc(s_moa, 1)

            def gap_exp(q):
                wait(act, s_gap, q + 1)
                act.activation(gap[:, :, 1], gap[:, :, 0], ACT.Exp).then_inc(s_ge, 1)

            def expert(q, pq, k):
                kind, e, f = EXPERT_PIECES[k]
                wait(act, s_mo, TP * q + TP_E + k + 1)
                src = mo[:, (TP * pq + TP_E + k) % 2]
                if kind == "gu":
                    wait(act, s_h, 2 * (NE * q + e) + f - 1)
                    act.activation(th[:, f, :], src[:, 0, :], ACT.Tanh, scale=0.5).then_inc(s_th, 1)
                else:
                    wait(act, s_acc, NE * q + e)
                    if e == 0:
                        wait(act, s_wts, q + 1)
                    rows = src.rearrange("p a (b d) -> p (a b) d", d=DM)
                    for i in range(NT):
                        last = act.activation(xf[:, i, :], rows[:, i, :], ACT.Copy, scale=wts[:, 1, i, e:e + 1])
                    last.then_inc(s_sc, 1)
                    act.wait_ge(s_sc, NE * q + e + 1)
                    act.sem_inc(s_moa, 1)

            def front_slot(q, pq, n):
                if n == 2:
                    take_x(q, pq)
                if n == 3:
                    take_z(q, pq)
                if n in (4, 5, 6, 7):
                    take_u(q, pq, n - 4)
                if n == 8:
                    silus(q, pq)
                if n == 9:
                    take_xd(q, pq)
                if n in (10, 11, 12, 13):
                    softplus(q, pq, n - 10)

            def step(q, pq, front, tail):
                scan = front is not None
                for n in range(UN):
                    if scan and n + 1 < UN:
                        unit(q, n + 1)
                    if front and n + 1 == UN:
                        unit(q + 1, 0)
                    if tail:
                        if n == 4:
                            take_xf(q - 1, 1 - pq)
                        if n == 5:
                            gap_exp(q - 1)
                    if front:
                        front_slot(q + 1, 1 - pq, n)
                    if tail:
                        for k in pieces(n):
                            expert(q - 1, 1 - pq, k)

            for n in range(UN):
                front_slot(0, 0, n)
            unit(0, 0)
            steps(act, step)

        @block.vector
        def _(dve):
            dve.wait_ge(s_w, 160)

            def moments(k, src, done, bn):
                for i in range(NT):
                    last = dve.bn_stats(stats[:, k, i, :], src[:, i, :])
                last.then_inc(s_bn, 1)
                dve.wait_ge(s_bn, bn)
                dve.sem_inc(s_agg, 1)
                for i in range(NT):
                    last = dve.bn_aggr(mv[:, k, i, :], stats[:, k, i, :])
                last.then_inc(done, 1)

            def norm_x(q, pq):
                wait(dve, s_rs, q + 1)
                wait(dve, s_fr, FT * (q - 1) + FT_X + DC)
                for i in range(NT):
                    last = dve.tensor_scalar(xn[:, i, :], xin[:, i, :], mv[:, 0, i, 0:1], rst[:, 0, i, 1:2], ALU.subtract, ALU.mult)
                last.then_inc(s_y, 1)
                dve.wait_ge(s_y, q + 1)
                dve.tensor_tensor(xs[:, pq], xin[:], xn[:], ALU.add).then_inc(s_xs, 1)
                dve.wait_ge(s_xs, q + 1)
                for i in range(NT):
                    last = dve.tensor_scalar(xn[:, i, :], xn[:, i, :], rst[:, 0, i, 3:4], None, ALU.mult)
                last.then_inc(s_xn, 1)

            def conv(q, pq, c):
                v = CC * q + c
                ub, dst = ubuf[:, c % 2, :], uc[:, pq, c, :]
                wait(dve, s_conv, v - 1)
                if pq == 0:
                    dve.memset(ub[:, 0:TAPS - 1], 0.0).then_inc(s_tap, 1)
                else:
                    dve.tensor_copy(ub[:, 0:TAPS - 1], halo[:, c, :]).then_inc(s_tap, 1)
                dve.wait_ge(s_tap, 4 * v + 1)
                wait(dve, s_u, v + 1)
                dve.tensor_scalar(dst, ub[:, 0:T], chan_s[:, c, 0:1], None, ALU.mult).then_inc(s_tap, 1)
                for k in range(1, TAPS):
                    dve.wait_ge(s_tap, 4 * v + 1 + k)
                    ins = dve.scalar_tensor_tensor(dst, ub[:, k:k + T], chan_s[:, c, k:k + 1], dst, ALU.mult, ALU.add)
                    if k < TAPS - 1:
                        ins.then_inc(s_tap, 1)
                dve.tensor_copy(halo[:, c, :], ub[:, T:T + TAPS - 1]).then_inc(s_conv, 1)

            def softplus(q, pq, c):
                v = CC * q + c
                wait(dve, s_abs, v + 1)
                wait(dve, s_dt, v)
                dve.tensor_scalar(t_m[:], fr[:, (FT * pq + FT_DT + c) % 2, :], chan_s[:, c, TAPS + 1:TAPS + 2], 0.0,
                                  ALU.add, ALU.max).then_inc(s_frd, 1)
                wait(dve, s_e, v + 1)
                dve.tensor_scalar(t_r[:], t_e[:], 1.0, 1.0, ALU.add, ALU.subtract).then_inc(s_m, 1)

            def unit(q, pq, n):
                c, g = n // G, n % G
                if c == 0:
                    wait(dve, s_bc[g], 128 * (q + 1))
                wait(dve, s_exp, UN * q + n + 1)
                wait(dve, s_dbu, UN * q + n + 1)
                for j in range(J):
                    init = 0.0 if pq == 0 else carry[:, n, j:j + 1]
                    last = dve.tensor_tensor_scan(dA[:, n % 2, j, :], dA[:, n % 2, j, :], dBu[:, n % 2, j, :], init,
                                                  ALU.mult, ALU.add)
                last.then_inc(s_scan, 1)

            def weigh(q, pq, n):
                g = n % G
                dve.wait_ge(s_scan, UN * q + n + 1)
                if pq == 0:
                    dve.tensor_copy(carry[:, n, :], dA[:, n % 2, :, T - 1]).then_inc(s_carry, 1)
                    dve.wait_ge(s_carry, UN // 2 * q + n + 1)
                dve.tensor_tensor(dA[:, n % 2], dA[:, n % 2], c_bc[:, g, :].unsqueeze(1).to_broadcast([P, J, T]),
                                  ALU.mult).then_inc(s_hc, 1)

            def gated(q, pq, c):
                wait(dve, s_ymm, UN * q + G * (c + 1))
                wait(dve, s_uc, CC * q + c + 1)
                dve.scalar_tensor_tensor(uc[:, pq, c, :], uc[:, pq, c, :], chan_s[:, c, TAPS + 2:TAPS + 3], yps[:, c % 2, :],
                                         ALU.mult, ALU.add).then_inc(s_yd, 1)
                dve.wait_ge(s_yd, CC * q + c + 1)
                wait(dve, s_sz, q + 1)
                dve.tensor_tensor(sz[:, pq, c, :], uc[:, pq, c, :], sz[:, pq, c, :], ALU.mult).then_inc(s_yg, 1)

            def residual(q, pq):
                wait(dve, s_mo, TP * q + TP_O + 1)
                wait(dve, s_out, 16 * q)
                rows = mo[:, (TP * pq + TP_O) % 2].rearrange("p a (b d) -> p (a b) d", d=DM)
                dve.tensor_tensor(x2[:], rows, xs[:, pq], ALU.add).then_inc(s_x2, 1)
                dve.wait_ge(s_x2, q + 1)
                dve.sem_inc(s_mod, 1)

            def norm_x2(q):
                wait(dve, s_rs2, q + 1)
                for i in range(NT):
                    last = dve.tensor_scalar(xf[:, i, :], x2[:, i, :], mv[:, 1, i, 0:1], rst[:, 1, i, 1:2], ALU.subtract, ALU.mult)
                last.then_inc(s_xf, 1)

            def route(q, pq):
                link = [LG * q]

                def then(ins):
                    ins.then_inc(s_lg, 1)
                    link[0] = link[0] + 1
                    dve.wait_ge(s_lg, link[0])

                wait(dve, s_mo, TP * q + TP_B + 1)
                src = mo[:, (TP * pq + TP_B) % 2, 0, 0:NT * NE].rearrange("p (i e) -> p i e", e=NE)
                then(dve.tensor_tensor(lg[:], src, rb_s[:].unsqueeze(1).to_broadcast([P, NT, NE]), ALU.add))
                dve.sem_inc(s_mod, 1)
                for i in range(NT):
                    last = dve.max(mx[:, i, :], lg[:, i, :])
                then(last)
                dve.tensor_tensor(gap[:, :, 0], mx[:, :, 1], mx[:, :, 0], ALU.subtract).then_inc(s_gap, 1)
                for i in range(NT):
                    last = dve.max_index(ix[:, i, :], mx[:, i, :], lg[:, i, :])
                then(last)
                then(dve.tensor_copy(ixf[:], ix[:, :, 0:2]))
                wait(dve, s_ge, q + 1)
                then(dve.tensor_scalar(gap[:, :, 2], gap[:, :, 1], 1.0, 2.0, ALU.add, ALU.mult))
                then(dve.reciprocal(gap[:, :, 2], gap[:, :, 2]))
                then(dve.tensor_tensor(gap[:, :, 3], gap[:, :, 2], gap[:, :, 1], ALU.mult))
                for i in range(NT):
                    for s in range(2):
                        last = dve.tensor_scalar(wts[:, s, i, :], iota, ixf[:, i, s:s + 1], gap[:, i, 2 + s:3 + s],
                                                 ALU.is_equal, ALU.mult)
                then(last)
                then(dve.tensor_copy(ixf[:], ix[:, :, 0:2]))
                dve.tensor_tensor(wts[:, 1], wts[:, 0], wts[:, 1], ALU.add).then_inc(s_wts, 1)

            def expert(q, pq, k):
                kind, e, f = EXPERT_PIECES[k]
                if kind == "down":
                    return
                v = 2 * (NE * q + e) + f + 1
                src = mo[:, (TP * pq + TP_E + k) % 2]
                wait(dve, s_th, v)
                dve.scalar_tensor_tensor(th[:, f, :], th[:, f, :], 1.0, src[:, 0, :], ALU.add, ALU.mult).then_inc(s_ga, 1)
                dve.wait_ge(s_ga, v)
                dve.tensor_tensor(hT[:, e % 2, f, :], th[:, f, :], src[:, 1, :], ALU.mult).then_inc(s_h, 1)
                dve.wait_ge(s_h, v)
                dve.sem_inc(s_mod, 1)

            def front_slot(q, pq, n, tails):
                if n == 0:
                    wait(dve, s_x, 16 * (q + 1))
                    moments(0, xin, s_mv, q + tails + 1)
                if n == 2:
                    norm_x(q, pq)
                if n in (4, 5, 6, 7):
                    conv(q, pq, n - 4)
                if n in (10, 11, 12, 13):
                    softplus(q, pq, n - 10)

            def step(q, pq, front, tail):
                scan = front is not None
                for n in range(UN):
                    if scan:
                        unit(q, pq, n)
                    if tail:
                        if n == 2:
                            residual(q - 1, 1 - pq)
                            moments(1, x2, s_mv2, (2 * q + 2 if front else NQ + q))
                        if n == 4:
                            norm_x2(q - 1)
                        if n == 5:
                            route(q - 1, 1 - pq)
                        for k in list(pieces(n))[:1]:
                            expert(q - 1, 1 - pq, k)
                    if scan:
                        weigh(q, pq, n)
                        if n % G == 0 and n:
                            gated(q, pq, n // G - 1)
                    if tail:
                        if n == 0:
                            gated(q - 1, 1 - pq, CC - 1)
                    if front:
                        front_slot(q + 1, 1 - pq, n, q - 1 if tail else 0)
                    if tail:
                        for k in list(pieces(n))[1:]:
                            expert(q - 1, 1 - pq, k)

            for n in range(UN):
                front_slot(0, 0, n, 0)
            steps(dve, step)

        @block.gpsimd
        def _(pool):
            pool.memset(xd[:], 0.0).then_inc(s_init, 1)
            pool.memset(nhalf[:], -0.5).then_inc(s_init, 1)
            pool.memset(eps[:], EPS).then_inc(s_init, 1)
            pool.wait_ge(s_init, 3)

            def deviation(k, q, mvs, done):
                wait(pool, mvs, q + 1)
                base = (2 * q if k == 0 else 0)
                s = s_pow if k == 0 else s_pow2
                n = 5 if k == 0 else 1
                pool.tensor_tensor(rst[:, k, :, 0], mv[:, k, :, 1], eps[:], ALU.add).then_inc(s, 1)
                pool.wait_ge(s, n * q + 1)
                ins = pool.tensor_tensor(rst[:, k, :, 1], rst[:, k, :, 0], nhalf[:], ALU.pow)
                if k == 1:
                    ins.then_inc(done, 1)
                    return
                ins.then_inc(s, 1)
                pool.wait_ge(s, n * q + 2)
                pool.tensor_tensor(rst[:, k, :, 2], rst[:, k, :, 1], rst[:, k, :, 1], ALU.mult).then_inc(s, 1)
                pool.wait_ge(s, n * q + 3)
                pool.tensor_tensor(rst[:, k, :, 2], rst[:, k, :, 2], mv[:, k, :, 1], ALU.mult).then_inc(s, 1)
                pool.wait_ge(s, n * q + 4)
                pool.tensor_tensor(rst[:, k, :, 2], rst[:, k, :, 2], eps[:], ALU.add).then_inc(s, 1)
                pool.wait_ge(s, n * q + 5)
                pool.tensor_tensor(rst[:, k, :, 3], rst[:, k, :, 2], nhalf[:], ALU.pow).then_inc(done, 1)

            def softplus(q, pq, c):
                v = CC * q + c
                wait(pool, s_m, v + 1)
                pool.tensor_tensor(t_r[:], t_e[:], t_r[:], ALU.subtract).then_inc(s_sp, 1)
                wait(pool, s_l, v + 1)
                pool.wait_ge(s_sp, 3 * v + 1)
                pool.tensor_tensor(t_r[:], t_r[:], dtb[:, c % 2, :], ALU.add).then_inc(s_sp, 1)
                pool.wait_ge(s_sp, 3 * v + 2)
                pool.tensor_tensor(dtb[:, c % 2, :], t_r[:], t_m[:], ALU.add).then_inc(s_sp, 1)
                pool.wait_ge(s_sp, 3 * v + 3)
                wait(pool, s_uc, v + 1)
                pool.tensor_tensor(dtub[:, c % 2, :], dtb[:, c % 2, :], uc[:, pq, c, :], ALU.mult).then_inc(s_dt, 1)

            def unit(q, n):
                c, g = n // G, n % G
                if g == 0:
                    wait(pool, s_rdtu[c % 2], 64 * (2 * q + c // 2 + 1))
                if c == 0:
                    wait(pool, s_bc[g], 128 * (q + 1))
                wait(pool, s_scan, UN * q + n - 1)
                pool.tensor_tensor(dBu[:, n % 2], rep_dtu[:, c % 2], b_bc[:, g, :].unsqueeze(1).to_broadcast([P, J, T]),
                                   ALU.mult).then_inc(s_dbu, 1)

            def add_expert(q, e):
                wait(pool, s_sc, NE * q + e + 1)
                if e:
                    wait(pool, s_acc, NE * q + e)
                pool.tensor_tensor(x2[:], x2[:], xf[:], ALU.add).then_inc(s_acc, 1)

            def step(q, pq, front, tail):
                scan = front is not None
                for n in range(UN):
                    if scan and n + 1 < UN:
                        unit(q, n + 1)
                    if front and n + 1 == UN:
                        unit(q + 1, 0)
                    if tail:
                        if n == 3:
                            deviation(1, q - 1, s_mv2, s_rs2)
                        for k in pieces(n - 1):
                            if EXPERT_PIECES[k][0] == "down":
                                add_expert(q - 1, EXPERT_PIECES[k][1])
                    if front:
                        if n == 1:
                            deviation(0, q + 1, s_mv, s_rs)
                        if n in (10, 11, 12, 13):
                            softplus(q + 1, 1 - pq, n - 10)

            deviation(0, 0, s_mv, s_rs)
            for c in range(CC):
                softplus(0, 0, c)
            unit(0, 0)
            steps(pool, step)


def program(nc, args):
    mamba_moe(nc, *args)


def kernel(**inputs):
    import concourse.bacc as bacc
    from concourse.bass_utils import run_bass_kernel_spmd

    i = {k[3:]: np.asarray(v) for k, v in inputs.items()}

    def rows(a, k):
        return a.reshape(k, P, -1).transpose(1, 0, 2)

    def cols(a, k):
        return a.reshape(k, P).T

    w_dt = np.zeros((P, DI), np.float32)
    w_dt[:RANK] = i["attn_W_dt"].T
    chan = np.concatenate([rows(i["attn_conv_w"], CC)] + [cols(i[n], CC)[:, :, None] for n in
                          ("attn_conv_b", "attn_b_dt", "attn_D")], axis=2)
    a_log = i["attn_A_log"].reshape(CC, J, 32, G, R).transpose(4, 2, 0, 3, 1).reshape(P, UN, J)
    moe = np.concatenate(
        [np.concatenate([i["ffn_we_gate"], i["ffn_we_up"]], axis=2).reshape(NE, DC, P, 2 * DM).transpose(0, 2, 1, 3).reshape(NE, P, -1),
         i["ffn_we_down"].reshape(NE, DC, P, DM).transpose(0, 2, 1, 3).reshape(NE, P, -1)], axis=2)
    lane = np.arange(P)
    consts = np.concatenate([np.eye(P), lane[:, None] % 32 == np.arange(32)[None, :],
                             np.tile(np.arange(NE), (P, 1))], axis=1).astype(np.float32)
    arrays = {
        "x": i["attn_x"],
        "w_in": rows(i["attn_W_in"].T, DC),
        "w_xp": rows(i["attn_W_xp"].T, CC),
        "w_dt": w_dt,
        "w_out": rows(i["attn_W_out"].T, CC),
        "w_moe": moe,
        "chan": chan,
        "a_log": a_log,
        "ln_gb": np.stack([cols(i["attn_ln_g"], DC), cols(i["attn_ln_b"], DC)], axis=1),
        "r_w": rows(i["ffn_router_w"], DC),
        "r_b": np.broadcast_to(i["ffn_router_b"], (P, NE)),
        "consts": consts,
    }
    arrays = {k: np.ascontiguousarray(v) for k, v in arrays.items()}
    nc = bacc.Bacc("TRN2", target_bir_lowering=False, num_devices=1)
    args = [nc.dram_tensor(f"in_{k}", a.shape, mybir.dt.from_np(a.dtype), kind="ExternalInput").ap()
            for k, a in arrays.items()]
    args.append(nc.dram_tensor("out_0", (BATCH, SEQ, DM), F32, kind="ExternalOutput").ap())
    order = ["x", "w_in", "w_xp", "w_dt", "w_out", "w_moe", "chan", "a_log", "ln_gb", "r_w", "r_b", "consts"]
    assert list(arrays) == order
    program(nc, args)
    r = run_bass_kernel_spmd(nc, [{f"in_{k}": a for k, a in arrays.items()}], core_ids=[0])
    return r.results[0]["out_0"]
```

```python
from contextlib import ExitStack

import numpy as np

import concourse.bass as bass
from concourse import mybir

F32 = mybir.dt.float32
U32 = mybir.dt.uint32
ALU = mybir.AluOpType
ACT = mybir.ActivationFunctionType
AX_X = mybir.AxisListType.X

P = 128
BATCH, SEQ, DM = 8, 1024, 256
DI, NS, TAPS, RANK = 512, 16, 4, 16
NE = 8
T = 512
NQ = BATCH * SEQ // T
NT = T // P
DC = DM // P
CC = DI // P
R = 4
G = NS // R
J = P // 32
UN = CC * G
EPS = 1e-5

NK = (NT * 2 * P) // P + NE - 1
SLOTS = NK * P

READER = {"O": "dve", "X": "act", "Z": "act", "F": "act", "U": "act", "R": "dve", "K": "dve", "V": "act", "D": "dve"}


def ring_order(front, tail):
    names = []
    names += ["O0", "O1"] if tail else []
    names += ["X0", "X1", "Z0", "Z1", "Z2", "Z3"] if front else []
    names += ["F0", "F1"] if tail else []
    names += ["U0"] if front else []
    names += ["R0"] if tail else []
    names += ["U1"] if front else []
    names += ["K0"] if tail else []
    names += ["U2", "U3", "V0", "D0", "D1", "D2", "D3"] if front else []
    return names


def ring_place(q, name):
    full = ring_order(True, True)
    count = {"act": sum(READER[n[0]] == "act" for n in full), "dve": sum(READER[n[0]] == "dve" for n in full)}
    alone = ring_order(True, False)
    heads = {"act": 2 * sum(READER[n[0]] == "act" for n in alone), "dve": 2 * sum(READER[n[0]] == "dve" for n in alone)}

    def flags(step):
        return (True, False) if step < 1 else (step < NQ - 1, step <= NQ)

    if isinstance(q, int):
        before = [n for step in range(-1, q) for n in ring_order(*flags(step))]
        names = ring_order(*flags(q))
        at = len(before) + names.index(name)
        if at < 2:
            return at % 2, at + 1, None
        seen = (before + names)[:at - 1]
        who = READER[seen[-1][0]]
        return at % 2, at + 1, (who, sum(READER[n[0]] == who for n in seen))
    k = full.index(name)
    seen = (full + full)[:len(full) + k - 1]
    who = READER[seen[-1][0]]
    number = len(full) * (q - 1) + 2 * len(alone) + k + 1
    released = count[who] * (q - 2) + heads[who] + sum(READER[n[0]] == who for n in seen)
    return None, number, (who, released)


def mamba_moe(nc, x, w_in, w_xp, w_dt, w_out, w_moe, chan, a_log, ln_gb, r_w, r_b, consts, out):
    with ExitStack() as ctx:
        def sb(name, shape, dt=F32):
            return ctx.enter_context(nc.sbuf_tensor(name, shape, dt))

        def sem(name):
            return ctx.enter_context(nc.semaphore(name))

        w_in_s = sb("w_in_s", [P, DC, 2 * DI])
        w_xp_s = sb("w_xp_s", [P, CC, RANK + 2 * NS])
        w_dt_s = sb("w_dt_s", [P, DI])
        w_out_s = sb("w_out_s", [P, CC, DM])
        chan_s = sb("chan_s", [P, CC, TAPS + 3])
        a_s = sb("a_s", [P, UN, J])
        ln_s = sb("ln_s", [P, 2, DC])
        rw_s = sb("rw_s", [P, DC, NE])
        rb_s = sb("rb_s", [P, NE])
        const_s = sb("const_s", [P, 3 * P + 32 + 2 * NE + NT + NK])
        ident = const_s[:, 0:P]
        sumsel = const_s[:, P:P + 32]
        before = const_s[:, P + 32:2 * P + 32]
        ones = const_s[:, 2 * P + 32:3 * P + 32]
        iota = const_s[:, 3 * P + 32:3 * P + 32 + NE]
        ones_e = const_s[:, 3 * P + 32 + NE:3 * P + 32 + 2 * NE]
        fills = const_s[:, 3 * P + 32 + 2 * NE:3 * P + 32 + 2 * NE + NT]
        iota_k = const_s[:, 3 * P + 32 + 2 * NE + NT:3 * P + 32 + 2 * NE + NT + NK]
        nhalf = sb("nhalf", [P, NT])
        eps = sb("eps", [P, NT])
        w_e = sb("w_e", [P, 2, DC * 2 * DM + 2 * DM])

        xin = sb("xin", [P, NT, DM])
        xs = sb("xs", [P, NT, DM])
        xn = sb("xn", [P, NT, DM])
        xnT = sb("xnT", [P, DC, T])
        stats = sb("stats", [P, 2, NT, 6])
        mv = sb("mv", [P, 2, NT, 2])
        rst = sb("rst", [P, 2, NT, 4])
        ubuf = sb("ubuf", [P, 2, T + TAPS - 1])
        halo = sb("halo", [P, CC, TAPS - 1])
        uc = sb("uc", [P, 2, CC, T])
        sz = sb("sz", [P, 2, CC, T])
        xd = sb("xd", [P, T])
        t_e = sb("t_e", [P, T])
        t_r = sb("t_r", [P, T])
        t_m = sb("t_m", [P, T])
        dtb = sb("dtb", [P, 2, T])
        dtub = sb("dtub", [P, 2, T])

        b_bc = sb("b_bc", [P, G, T])
        c_bc = sb("c_bc", [P, G, T])
        rep_dt = sb("rep_dt", [P, 2, J, T])
        rep_dtu = sb("rep_dtu", [P, 2, J, T])
        dA = sb("dA", [P, 2, J, T])
        dBu = sb("dBu", [P, 2, J, T])
        carry = sb("carry", [P, UN, J])

        x2 = sb("x2", [P, NT, DM])
        xf = sb("xf", [P, NT, DM])
        xfT = sb("xfT", [P, DC, T])
        lg = sb("lg", [P, NT, NE])
        mx = sb("mx", [P, NT, 8])
        ix = sb("ix", [P, NT, 8], U32)
        ixf = sb("ixf", [P, NT, 2])
        gap = sb("gap", [P, NT, 2])
        w12 = sb("w12", [P, 2, 2, NT])
        hot = sb("hot", [P, 3, NT, NE])
        r5 = sb("r5", [P, NT + 1, NE])
        fill = sb("fill", [P, NE, NT])
        ntile = sb("ntile", [P, NE])
        end = sb("end", [P, NE])
        start = sb("start", [P, NE])
        row = sb("row", [P, NT, NE])
        row2 = sb("row2", [P, 2, NT, NE])
        posf = sb("posf", [P, 2, NT])
        pos = sb("pos", [P, 2, 2, NT], U32)
        past = sb("past", [P, NK, NE])
        tef = sb("tef", [P, NK])
        te = sb("te", [P, 2, NK], U32)

        xt = sb("xt", [P, 2, DM])
        xtT = sb("xtT", [P, 2, DC, P])
        th = sb("th", [P, 2, DM])
        hT = sb("hT", [P, 2, DC, P])
        yt = sb("yt", [P, 2, DM])
        pair = xfT[:, :, :].rearrange("p c (s d) -> p c s d", d=DM)
        xr = sb("xr", [P, 2, DM])

        ring = ctx.enter_context(nc.psum_tensor("ring", [P, 2, 512], F32))
        yps = ctx.enter_context(nc.psum_tensor("yps", [P, 2, 512], F32))
        p_a = ctx.enter_context(nc.psum_tensor("p_a", [P, 512], F32))
        p_g = ctx.enter_context(nc.psum_tensor("p_g", [P, 512], F32))
        p_h = ctx.enter_context(nc.psum_tensor("p_h", [P, 512], F32))
        p_d = ctx.enter_context(nc.psum_tensor("p_d", [P, 512], F32))

        bc_d = nc.dram_tensor("bc_d", (2 * NS, T), F32, kind="Internal").ap()
        dt_d = nc.dram_tensor("dt_d", (2, 2, CC, P, T), F32, kind="Internal").ap()
        xs_d = nc.dram_tensor("xs_d", (2, P, NT, DM), F32, kind="Internal").ap()
        x2_d = nc.dram_tensor("x2_d", (2, P, NT, DM), F32, kind="Internal").ap()
        sorted_x = [nc.dram_tensor(f"sorted_x{i}", (SLOTS, DM), F32, kind="Internal").ap() for i in range(2)]
        sorted_y = [nc.dram_tensor(f"sorted_y{i}", (SLOTS, DM), F32, kind="Internal").ap() for i in range(2)]

        s_w = sem("s_w")
        s_init = sem("s_init")
        s_a = sem("s_a")
        s_x = sem("s_x")
        s_xs = sem("s_xs")
        s_bn = sem("s_bn")
        s_agg = sem("s_agg")
        s_mv = sem("s_mv")
        s_rs = sem("s_rs")
        s_pow = sem("s_pow")
        s_y = sem("s_y")
        s_xn = sem("s_xn")
        s_ring = sem("s_ring")
        s_ract = sem("s_ract")
        s_rdve = sem("s_rdve")
        s_xnT = sem("s_xnT")
        s_u = sem("s_u")
        s_tap = sem("s_tap")
        s_conv = sem("s_conv")
        s_uc = sem("s_uc")
        s_z = sem("s_z")
        s_sz = sem("s_sz")
        s_xd = sem("s_xd")
        s_bcw = sem("s_bcw")
        s_abs = sem("s_abs")
        s_e = sem("s_e")
        s_l = sem("s_l")
        s_m = sem("s_m")
        s_sp = sem("s_sp")
        s_dt = sem("s_dt")
        s_dtw = [sem(f"s_dtw{i}") for i in range(2)]
        s_bc = [sem(f"s_bc{g}") for g in range(G)]
        s_rdt = [sem(f"s_rdt{i}") for i in range(2)]
        s_rdtu = [sem(f"s_rdtu{i}") for i in range(2)]
        s_exp = sem("s_exp")
        s_dbu = sem("s_dbu")
        s_scan = sem("s_scan")
        s_carry = sem("s_carry")
        s_hc = sem("s_hc")
        s_ymm = sem("s_ymm")
        s_yd = sem("s_yd")
        s_yg = sem("s_yg")
        s_zero = sem("s_zero")
        s_xsw = sem("s_xsw")
        s_x2r = sem("s_x2r")
        s_x2 = sem("s_x2")
        s_x2w = sem("s_x2w")
        s_mv2 = sem("s_mv2")
        s_rs2 = sem("s_rs2")
        s_pow2 = sem("s_pow2")
        s_xf = sem("s_xf")
        s_xfT = sem("s_xfT")
        s_lg = sem("s_lg")
        s_gap = sem("s_gap")
        s_ge = sem("s_ge")
        s_hot = sem("s_hot")
        s_place = sem("s_place")
        s_pos = sem("s_pos")
        s_past = sem("s_past")
        s_te = sem("s_te")
        s_free = sem("s_free")
        s_sct = sem("s_sct")
        s_xt = [sem(f"s_xt{i}") for i in range(2)]
        s_wgu = [sem(f"s_wgu{i}") for i in range(2)]
        s_wdn = [sem(f"s_wdn{i}") for i in range(2)]
        s_ta = sem("s_ta")
        s_tg = sem("s_tg")
        s_th = sem("s_th")
        s_td = sem("s_td")
        s_xtT = sem("s_xtT")
        s_tanh = sem("s_tanh")
        s_ga = sem("s_ga")
        s_h = sem("s_h")
        s_hT = sem("s_hT")
        s_yt = sem("s_yt")
        s_ys = [sem(f"s_ys{i}") for i in range(2)]
        s_xr = [sem(f"s_xr{i}") for i in range(2)]
        s_pair = [sem(f"s_pair{i}") for i in range(2)]
        s_mix = sem("s_mix")
        s_comb = sem("s_comb")
        s_out = [sem(f"s_out{i}") for i in range(2)]
        LG, PL = 8, 9

        x_v = x.rearrange("b (h i p) d -> (b h) p i d", h=SEQ // T, p=P)
        out_v = out.rearrange("b (h i p) d -> (b h) p i d", h=SEQ // T, p=P)

        def chunk(v, q):
            return v[q] if isinstance(q, int) else v[bass.ds(q, 1)].rearrange("a p i d -> p (a i) d")

        def wait(eng, s, value):
            if isinstance(value, int) and value <= 0:
                return
            eng.wait_ge(s, value)

        def counts(eng, *values):
            return [v if isinstance(v, int) else eng.snap(eng.to_reg(v), min_val=0, max_val=1 << 15) for v in values]

        def steps(eng, step):
            step(0, 0, True, False, False, True)
            step(1, 1, True, True, False, True)
            step(2, 0, True, True, True, True)
            with eng.Fori(1, (NQ - 2) // 2) as i:
                step(i * 2 + 1, 1, True, True, True, True)
                step(i * 2 + 2, 0, True, True, True, True)
            step(NQ - 1, 1, False, True, True, True)
            step(NQ, 0, False, True, True, False)
            step(NQ + 1, 1, False, False, True, False)

        START = 8

        def positions(q, pq, n, tail, old):
            found = []
            if old and n + UN - START <= NK + 3:
                found.append((q - 2, pq, n + UN - START))
            if tail and n >= START:
                found.append((q - 1, 1 - pq, n - START))
            return found

        def tiles_even(q, pq, k):
            return 8 * NK * (q - pq) + 16 * ((NK * pq + k) // 2 + 1)

        DT_SLOTS = (10, 12, 14, 15)

        def place_of(q, pq, name):
            bank, number, release = ring_place(q, name)
            if bank is None:
                bank = ring_place(2 + pq, name)[0]
            return ring[:, bank, :], number, release

        block = ctx.enter_context(nc.Block())

        @block.sync
        def _(sp):
            for dst, src in ((w_in_s, w_in), (w_xp_s, w_xp), (w_dt_s, w_dt), (w_out_s, w_out), (chan_s, chan),
                             (a_s, a_log), (ln_s, ln_gb), (rw_s, r_w), (rb_s, r_b), (const_s, consts)):
                sp.dma_start(dst[:], src).then_inc(s_w, 16)

            def number(q):
                return q if isinstance(q, int) else sp.snap(q, min_val=0, max_val=NQ - 1)

            def load_x(q):
                at = number(q)
                wait(sp, s_xs, q)
                sp.dma_start(xin[:], chunk(x_v, at)).then_inc(s_x, 16)

            def store_bc(q):
                wait(sp, s_xd, q + 1)
                sp.dma_start(bc_d, xd[RANK:RANK + 2 * NS, :]).then_inc(s_bcw, 16)

            def load_bc(q, g):
                stored, used = counts(sp, 16 * q + 16, UN * q - G + g + 1)
                wait(sp, s_bcw, stored)
                wait(sp, s_dbu, used)
                wait(sp, s_hc, used)
                for dst, row in ((b_bc, 0), (c_bc, NS)):
                    for r in range(R):
                        src = bc_d[row + R * g + r:row + R * g + r + 1, :].to_broadcast([32, T])
                        sp.dma_start(dst[32 * r:32 * r + 32, g, :], src).then_inc(s_bc[g], 16)

            def store_dt(q, pq, c):
                wait(sp, s_dt, CC * q + c + 1)
                sp.dma_start(dt_d[pq, 0, c], dtb[:, c % 2, :]).then_inc(s_dtw[c % 2], 16)
                sp.dma_start(dt_d[pq, 1, c], dtub[:, c % 2, :]).then_inc(s_dtw[c % 2], 16)

            def load_rep(q, pq, c):
                stored, used = counts(sp, 32 * (2 * q + c // 2 + 1), G * (CC * q + c - 1))
                wait(sp, s_dtw[c % 2], stored)
                wait(sp, s_exp, used)
                wait(sp, s_dbu, used)
                for k, (dst, s) in enumerate(((rep_dt, s_rdt), (rep_dtu, s_rdtu))):
                    src = dt_d[pq, k, c].rearrange("(j d) t -> d j t", j=J)
                    for r in range(R):
                        sp.dma_start(dst[32 * r:32 * r + 32, c % 2], src).then_inc(s[c % 2], 16)

            def store_xs(q, pq):
                wait(sp, s_xs, q + 1)
                sp.dma_start(xs_d[pq], xs[:]).then_inc(s_xsw, 16)

            def load_x2(q, pq):
                stored, free = counts(sp, 16 * q + 16, 16 * q)
                wait(sp, s_xsw, stored)
                wait(sp, s_x2w, free)
                wait(sp, s_xf, q)
                sp.dma_start(x2[:], xs_d[pq]).then_inc(s_x2r, 16)

            def store_x2(q, pq):
                wait(sp, s_x2, 2 * q + 2)
                sp.dma_start(x2_d[pq], x2[:]).then_inc(s_x2w, 16)

            def load_tile(q, pq, k):
                v, b = NK * q + k, (pq + k) % 2
                scattered, routed, transposed = counts(sp, 32 * NT * (q + 1), q + 1, v - 1)
                if k == 0:
                    wait(sp, s_te, routed)
                    wait(sp, s_sct, scattered)
                wait(sp, s_ta, transposed)
                sp.dma_start(xt[:, b, :], sorted_x[pq][k * P:(k + 1) * P, :]).then_inc(s_xt[b], 16)
                load_expert(q, pq, k, v, s_tg, s_wgu[b], 0, DC * 2 * DM)

            def load_expert(q, pq, k, v, used, done, lo, hi):
                e = sp.value_load(te[0:1, pq, k:k + 1], min_val=0, max_val=NE - 1)
                wait(sp, used, v - 1)
                sp.dma_start(w_e[:, (pq + k) % 2, lo:hi],
                             w_moe[bass.ds(e, 1), :, lo:hi].rearrange("a p n -> p (a n)")).then_inc(done, 16)

            def store_tile(q, pq, k):
                wait(sp, s_yt, NK * q + k + 1)
                sp.dma_start(sorted_y[pq][k * P:(k + 1) * P, :], yt[:, (pq + k) % 2, :]).then_inc(s_ys[(pq + k) % 2], 16)

            def load_xr(q, pq, i):
                wait(sp, s_out[i % 2], 16 * (2 * q + i // 2))
                sp.dma_start(xr[:, i % 2, :], x2_d[pq, :, i, :]).then_inc(s_xr[i % 2], 16)

            def store_out(q, i):
                at = number(q)
                wait(sp, s_comb, NT * q + i + 1)
                dst = out_v[q] if isinstance(q, int) else out_v[bass.ds(at, 1)].rearrange("a p i d -> p (a i) d")
                sp.dma_start(dst[:, i, :], xr[:, i % 2, :]).then_inc(s_out[i % 2], 16)

            def step(q, pq, front, tail, old, scan):
                if scan:
                    load_rep(q, pq, 1)
                if front:
                    load_x(q + 1)
                if tail:
                    load_x2(q - 1, 1 - pq)
                for n in range(UN):
                    if scan and n == 4:
                        load_rep(q, pq, 2)
                    if scan and n == 8:
                        load_rep(q, pq, 3)
                    if front and n == 3:
                        store_xs(q + 1, 1 - pq)
                    if tail and n == 3:
                        store_x2(q - 1, 1 - pq)
                    if front and n == 10:
                        store_bc(q + 1)
                    if front and n in (11, 13, 15):
                        store_dt(q + 1, 1 - pq, (n - 11) // 2)
                        if n == 13:
                            load_rep(q + 1, 1 - pq, 0)
                    if front and n >= 13:
                        load_bc(q + 1, n - 13)
                    if old and n in (11, 13):
                        for i in ((0, 1) if n == 11 else (2, 3)):
                            load_xr(q - 2, pq, i)
                    if old and n in (12, 14):
                        for i in ((0, 1) if n == 12 else (2, 3)):
                            store_out(q - 2, i)
                    for c, pc, at in positions(q, pq, n, tail, old):
                        if 4 <= at < NK + 4:
                            store_tile(c, pc, at - 4)
                        if 1 <= at < NK + 1:
                            k = at - 1
                            load_expert(c, pc, k, NK * c + k, s_td, s_wdn[(pc + k) % 2], DC * 2 * DM, DC * 3 * DM)
                        if at + 1 < NK:
                            load_tile(c, pc, at + 1)
                    if tail and n == START - 1:
                        load_tile(q - 1, 1 - pq, 0)
                if front:
                    store_dt(q + 1, 1 - pq, 3)
                    load_bc(q + 1, G - 1)

            sp.wait_ge(s_init, 4)
            for i in range(2):
                sp.dma_start(sorted_x[i].rearrange("(k p) d -> p k d", p=P), xf[:, 0:1, :].to_broadcast([P, NK, DM])).then_inc(s_zero, 16)
            sp.wait_ge(s_zero, 32)
            load_x(0)
            store_xs(0, 0)
            store_bc(0)
            for g in range(G):
                load_bc(0, g)
            for c in range(CC):
                store_dt(0, 0, c)
            load_rep(0, 0, 0)
            steps(sp, step)
            for i in range(2):
                sp.wait_ge(s_out[i], 16 * NQ * NT // 2)

        @block.tensor
        def _(pe):
            pe.wait_ge(s_w, 160)
            pe.wait_ge(s_init, 4)

            def ring_tile(q, pq, name):
                bank, _, release = place_of(q, pq, name)
                if release:
                    wait(pe, s_ract if release[0] == "act" else s_rdve, release[1])
                return bank


            def transpose_x(q, pq):
                for c in range(DC):
                    dst = ring_tile(q, pq, f"X{c}")
                    wait(pe, s_xn, q + 2)
                    for i in range(NT):
                        last = pe.transpose(dst[:, i * P:(i + 1) * P], xn[:, i, c * P:(c + 1) * P], ident)
                    last.then_inc(s_ring, 1)

            def in_proj(q, pq, name, ch):
                dst = ring_tile(q, pq, name)
                wait(pe, s_xnT, DC * (q + 2))
                for c in range(DC):
                    last = pe.matmul(dst, w_in_s[:, c, ch * P:(ch + 1) * P], xnT[:, c, :], start=c == 0, stop=c == DC - 1)
                last.then_inc(s_ring, 1)

            def x_proj(q, pq):
                dst = ring_tile(q, pq, "V0")
                wait(pe, s_uc, CC * (q + 2))
                for c in range(CC):
                    last = pe.matmul(dst[0:RANK + 2 * NS, :], w_xp_s[:, c, :], uc[:, 1 - pq, c, :], start=c == 0, stop=c == CC - 1)
                last.then_inc(s_ring, 1)

            def dt_proj(q, pq, c):
                dst = ring_tile(q, pq, f"D{c}")
                wait(pe, s_xd, q + 2)
                pe.matmul(dst, w_dt_s[:, c * P:(c + 1) * P], xd[:], start=True, stop=True).then_inc(s_ring, 1)

            def unit(q, n):
                c, g = n // G, n % G
                if g == 0:
                    wait(pe, s_yg, CC * q + c - 1)
                wait(pe, s_hc, UN * q + n + 1)
                for j in range(J):
                    last = pe.matmul(yps[32 * j:32 * j + 32, c % 2, :], sumsel, dA[:, n % 2, j, :],
                                     start=g == 0, stop=g == G - 1)
                last.then_inc(s_ymm, 1)

            def out_proj(q, pq):
                for a in range(2):
                    dst = ring_tile(q, pq, f"O{a}")
                    wait(pe, s_yg, CC * q)
                    for i in range(2 * a, 2 * a + 2):
                        for c in range(CC):
                            last = pe.matmul(dst[:, i % 2 * DM:i % 2 * DM + DM], sz[:, 1 - pq, c, i * P:(i + 1) * P],
                                             w_out_s[:, c, :], start=c == 0, stop=c == CC - 1)
                    last.then_inc(s_ring, 1)

            def transpose_xf(q, pq):
                for c in range(DC):
                    dst = ring_tile(q, pq, f"F{c}")
                    wait(pe, s_xf, q)
                    for i in range(NT):
                        last = pe.transpose(dst[:, i * P:(i + 1) * P], xf[:, i, c * P:(c + 1) * P], ident)
                    last.then_inc(s_ring, 1)

            def router(q, pq):
                dst = ring_tile(q, pq, "R0")
                wait(pe, s_xfT, DC * q)
                for i in range(NT):
                    for c in range(DC):
                        last = pe.matmul(dst[:, i * NE:(i + 1) * NE], xfT[:, c, i * P:(i + 1) * P], rw_s[:, c, :],
                                         start=c == 0, stop=c == DC - 1)
                last.then_inc(s_ring, 1)

            def ranks(q, pq):
                dst = ring_tile(q, pq, "K0")
                wait(pe, s_hot, q)
                pe.matmul(dst[:, 0:NT * NE], before, hot[:, 2], start=True, stop=False, skip_group_check=True)
                for i in range(NT):
                    later = NT - i
                    last = pe.matmul(dst[:, (i + 1) * NE:(NT + 1) * NE].rearrange("p (i e) -> p i e", e=NE), ones,
                                     hot[:, 2, i:i + 1, :].to_broadcast([P, later, NE]),
                                     start=False, stop=i == NT - 1, skip_group_check=True)
                last.then_inc(s_ring, 1)

            def tile_transpose(q, pq, k):
                v, b = NK * q + k, (pq + k) % 2
                wait(pe, s_xt[b], tiles_even(q, pq, k))
                wait(pe, s_xtT, v)
                for c in range(DC):
                    last = pe.transpose(p_a[:, c * P:(c + 1) * P], xt[:, b, c * P:(c + 1) * P], ident)
                last.then_inc(s_ta, 1)

            def gate_up(q, pq, k):
                v, b = NK * q + k, (pq + k) % 2
                wait(pe, s_xtT, v + 1)
                wait(pe, s_wgu[b], tiles_even(q, pq, k))
                wait(pe, s_h, v)
                for c in range(DC):
                    last = pe.matmul(p_g[:], xtT[:, b, c, :], w_e[:, b, c * 2 * DM:(c + 1) * 2 * DM], start=c == 0, stop=c == DC - 1)
                last.then_inc(s_tg, 1)

            def h_transpose(q, pq, k):
                v, b = NK * q + k, (pq + k) % 2
                wait(pe, s_h, v + 1)
                wait(pe, s_hT, v)
                for c in range(DC):
                    last = pe.transpose(p_h[:, c * P:(c + 1) * P], th[:, b, c * P:(c + 1) * P], ident)
                last.then_inc(s_th, 1)

            def down(q, pq, k):
                v, b = NK * q + k, (pq + k) % 2
                wait(pe, s_hT, v + 1)
                wait(pe, s_wdn[b], tiles_even(q, pq, k))
                wait(pe, s_yt, v)
                for c in range(DC):
                    col = DC * 2 * DM + c * DM
                    last = pe.matmul(p_d[:, 0:DM], hT[:, b, c, :], w_e[:, b, col:col + DM], start=c == 0, stop=c == DC - 1)
                last.then_inc(s_td, 1)

            def front_slot(q, pq, n):
                if n == 2:
                    transpose_x(q, pq)
                if n == 3:
                    for c in range(CC):
                        in_proj(q, pq, f"Z{c}", CC + c)
                if n in (4, 5, 6, 7):
                    in_proj(q, pq, f"U{n - 4}", n - 4)
                if n == 9:
                    x_proj(q, pq)
                if n in DT_SLOTS:
                    dt_proj(q, pq, DT_SLOTS.index(n))

            def step(q, pq, front, tail, old, scan):
                for n in range(UN):
                    if n and scan:
                        unit(q, n - 1)
                    if n == 0 and tail:
                        unit(q - 1, UN - 1)
                    if tail:
                        if n == 1:
                            out_proj(q, pq)
                        if n == 4:
                            transpose_xf(q, pq)
                        if n == 5:
                            router(q, pq)
                        if n == 6:
                            ranks(q, pq)
                    if front:
                        front_slot(q, pq, n)
                    for c, pc, at in positions(q, pq, n, tail, old):
                        if 0 <= at - 3 < NK:
                            down(c, pc, at - 3)
                        if 0 <= at - 2 < NK:
                            h_transpose(c, pc, at - 2)
                        if 0 <= at - 1 < NK:
                            gate_up(c, pc, at - 1)
                        if at < NK:
                            tile_transpose(c, pc, at)

            for n in range(UN):
                front_slot(-1, 1, n)
            steps(pe, step)

        @block.scalar
        def _(act):
            act.wait_ge(s_w, 160)
            act.activation(a_s[:], a_s[:], ACT.Exp).then_inc(s_a, 1)
            act.wait_ge(s_a, 1)
            act.activation(a_s[:], a_s[:], ACT.Copy, scale=-1.0).then_inc(s_a, 1)
            act.wait_ge(s_a, 2)


            def ring_tile(q, pq, name):
                bank, number, _ = place_of(q, pq, name)
                wait(act, s_ring, number)
                return bank

            def take_x(q, pq):
                for c in range(DC):
                    src = ring_tile(q, pq, f"X{c}")
                    act.activation(xnT[:, c, :], src, ACT.Identity,
                                   scale=ln_s[:, 0, c:c + 1], bias=ln_s[:, 1, c:c + 1]).then_inc(s_xnT, 1)
                    act.wait_ge(s_xnT, DC * (q + 1) + c + 1)
                    act.sem_inc(s_ract, 1)

            def take_z(q, pq):
                for c in range(CC):
                    src = ring_tile(q, pq, f"Z{c}")
                    act.activation(sz[:, 1 - pq, c, :], src, ACT.Copy).then_inc(s_z, 1)
                    act.wait_ge(s_z, CC * (q + 1) + c + 1)
                    act.sem_inc(s_ract, 1)

            def take_u(q, pq, c):
                src = ring_tile(q, pq, f"U{c}")
                wait(act, s_conv, CC * (q + 1) + c - 1)
                act.activation(ubuf[:, c % 2, TAPS - 1:], src, ACT.Copy).then_inc(s_u, 1)
                act.wait_ge(s_u, CC * (q + 1) + c + 1)
                act.sem_inc(s_ract, 1)

            def silus(q, pq):
                act.activation(sz[:, 1 - pq], sz[:, 1 - pq], ACT.Silu).then_inc(s_sz, 1)
                for c in range(CC):
                    wait(act, s_conv, CC * (q + 1) + c + 1)
                    act.activation(uc[:, 1 - pq, c, :], uc[:, 1 - pq, c, :], ACT.Silu,
                                   bias=chan_s[:, c, TAPS:TAPS + 1]).then_inc(s_uc, 1)

            def take_xd(q, pq):
                src = ring_tile(q, pq, "V0")
                wait(act, s_bcw, 16 * (q + 1))
                n = RANK + 2 * NS
                act.activation(xd[0:n, :], src[0:n, :], ACT.Copy).then_inc(s_xd, 1)
                act.wait_ge(s_xd, q + 2)
                act.sem_inc(s_ract, 1)

            def softplus(q, pq, c):
                v = CC * (q + 1) + c
                src = ring_tile(q, pq, f"D{c}")
                wait(act, s_dt, v)
                act.activation(t_e[:], src, ACT.Abs, bias=chan_s[:, c, TAPS + 1:TAPS + 2]).then_inc(s_abs, 1)
                act.wait_ge(s_abs, v + 1)
                act.activation(t_e[:], t_e[:], ACT.Exp, scale=-1.0).then_inc(s_e, 1)
                act.wait_ge(s_e, v + 1)
                wait(act, s_dtw[c % 2], 32 * (2 * (q + 1) + c // 2))
                act.activation(dtb[:, c % 2, :], t_e[:], ACT.Ln, bias=1.0).then_inc(s_l, 1)

            def unit(q, n):
                c = n // G
                if n % G == 0:
                    wait(act, s_rdt[c % 2], 64 * (2 * q + c // 2 + 1))
                wait(act, s_ymm, UN * q + n - 1)
                for j in range(J):
                    last = act.activation(dA[:, n % 2, j, :], rep_dt[:, c % 2, j, :], ACT.Exp, scale=a_s[:, n, j:j + 1])
                last.then_inc(s_exp, 1)

            def take_xf(q, pq):
                for c in range(DC):
                    src = ring_tile(q, pq, f"F{c}")
                    act.activation(xfT[:, c, :], src, ACT.Copy).then_inc(s_xfT, 1)
                    act.wait_ge(s_xfT, DC * (q - 1) + c + 1)
                    act.sem_inc(s_ract, 1)

            def gap_exp(q):
                wait(act, s_gap, q)
                act.activation(gap[:, :, 1], gap[:, :, 0], ACT.Exp).then_inc(s_ge, 1)

            def take_tile(q, pq, k):
                v, b = NK * q + k, (pq + k) % 2
                wait(act, s_ta, v + 1)
                wait(act, s_tg, v - 1)
                act.activation(xtT[:, b], p_a[:, 0:DM].rearrange("p (c t) -> p c t", t=P), ACT.Copy).then_inc(s_xtT, 1)

            def tanh(q, pq, k):
                v, b = NK * q + k, (pq + k) % 2
                wait(act, s_tg, v + 1)
                wait(act, s_th, v - 1)
                act.activation(th[:, b, :], p_g[:, 0:DM], ACT.Tanh, scale=0.5).then_inc(s_tanh, 1)

            def take_h(q, pq, k):
                v, b = NK * q + k, (pq + k) % 2
                wait(act, s_th, v + 1)
                wait(act, s_td, v - 1)
                act.activation(hT[:, b], p_h[:, 0:DM].rearrange("p (c t) -> p c t", t=P), ACT.Copy).then_inc(s_hT, 1)

            def take_y(q, pq, k):
                v, b = NK * q + k, (pq + k) % 2
                wait(act, s_td, v + 1)
                wait(act, s_ys[b], tiles_even(q, pq, k - 2))
                act.activation(yt[:, b, :], p_d[:, 0:DM], ACT.Copy).then_inc(s_yt, 1)

            def front_slot(q, pq, n):
                if n == 2:
                    take_x(q, pq)
                if n == 3:
                    take_z(q, pq)
                if n in (4, 5, 6, 7):
                    take_u(q, pq, n - 4)
                if n == 8:
                    silus(q, pq)
                if n == 9:
                    take_xd(q, pq)
                if n in DT_SLOTS:
                    softplus(q, pq, DT_SLOTS.index(n))

            def step(q, pq, front, tail, old, scan):
                for n in range(UN):
                    if scan and n + 1 < UN:
                        unit(q, n + 1)
                    if front and n + 1 == UN:
                        unit(q + 1, 0)
                    if tail:
                        if n == 4:
                            take_xf(q, pq)
                        if n == 5:
                            gap_exp(q)
                    if front:
                        front_slot(q, pq, n)
                    for c, pc, at in positions(q, pq, n, tail, old):
                        if 0 <= at - 3 < NK:
                            take_y(c, pc, at - 3)
                        if 0 <= at - 2 < NK:
                            take_h(c, pc, at - 2)
                        if 0 <= at - 1 < NK:
                            tanh(c, pc, at - 1)
                        if at < NK:
                            take_tile(c, pc, at)

            for n in range(UN):
                front_slot(-1, 1, n)
            unit(0, 0)
            steps(act, step)

        @block.vector
        def _(dve):
            dve.wait_ge(s_w, 160)

            def moments(k, src, done, bn):
                for i in range(NT):
                    last = dve.bn_stats(stats[:, k, i, :], src[:, i, :])
                last.then_inc(s_bn, 1)
                dve.wait_ge(s_bn, bn)
                dve.sem_inc(s_agg, 1)
                for i in range(NT):
                    last = dve.bn_aggr(mv[:, k, i, :], stats[:, k, i, :])
                last.then_inc(done, 1)

            def norm_x(q, pq):
                wait(dve, s_rs, q + 1)
                wait(dve, s_xnT, DC * q)
                wait(dve, s_xsw, 16 * q)
                for i in range(NT):
                    last = dve.tensor_scalar(xn[:, i, :], xin[:, i, :], mv[:, 0, i, 0:1], rst[:, 0, i, 1:2], ALU.subtract, ALU.mult)
                last.then_inc(s_y, 1)
                dve.wait_ge(s_y, q + 1)
                dve.tensor_tensor(xs[:], xin[:], xn[:], ALU.add).then_inc(s_xs, 1)
                dve.wait_ge(s_xs, q + 1)
                for i in range(NT):
                    last = dve.tensor_scalar(xn[:, i, :], xn[:, i, :], rst[:, 0, i, 3:4], None, ALU.mult)
                last.then_inc(s_xn, 1)

            def conv(q, pq, c):
                v = CC * q + c
                ub, dst = ubuf[:, c % 2, :], uc[:, pq, c, :]
                wait(dve, s_conv, v - 1)
                if pq == 0:
                    dve.memset(ub[:, 0:TAPS - 1], 0.0).then_inc(s_tap, 1)
                else:
                    dve.tensor_copy(ub[:, 0:TAPS - 1], halo[:, c, :]).then_inc(s_tap, 1)
                dve.wait_ge(s_tap, 4 * v + 1)
                wait(dve, s_u, v + 1)
                dve.tensor_scalar(dst, ub[:, 0:T], chan_s[:, c, 0:1], None, ALU.mult).then_inc(s_tap, 1)
                for k in range(1, TAPS):
                    dve.wait_ge(s_tap, 4 * v + 1 + k)
                    ins = dve.scalar_tensor_tensor(dst, ub[:, k:k + T], chan_s[:, c, k:k + 1], dst, ALU.mult, ALU.add)
                    if k < TAPS - 1:
                        ins.then_inc(s_tap, 1)
                dve.tensor_copy(halo[:, c, :], ub[:, T:T + TAPS - 1]).then_inc(s_conv, 1)

            def softplus(q, pq, c):
                v = CC * q + c
                wait(dve, s_abs, v + 1)
                wait(dve, s_dt, v)
                dve.tensor_scalar(t_m[:], place_of(q - 1, 1 - pq, f"D{c}")[0], chan_s[:, c, TAPS + 1:TAPS + 2], 0.0,
                                  ALU.add, ALU.max).then_inc(s_rdve, 1)
                wait(dve, s_e, v + 1)
                dve.tensor_scalar(t_r[:], t_e[:], 1.0, 1.0, ALU.add, ALU.subtract).then_inc(s_m, 1)

            def unit(q, pq, n):
                c, g = n // G, n % G
                if c == 0:
                    wait(dve, s_bc[g], 128 * (q + 1))
                wait(dve, s_exp, UN * q + n + 1)
                wait(dve, s_dbu, UN * q + n + 1)
                for j in range(J):
                    init = 0.0 if pq == 0 else carry[:, n, j:j + 1]
                    last = dve.tensor_tensor_scan(dA[:, n % 2, j, :], dA[:, n % 2, j, :], dBu[:, n % 2, j, :], init,
                                                  ALU.mult, ALU.add)
                last.then_inc(s_scan, 1)

            def weigh(q, pq, n):
                g = n % G
                dve.wait_ge(s_scan, UN * q + n + 1)
                if pq == 0:
                    dve.tensor_copy(carry[:, n, :], dA[:, n % 2, :, T - 1]).then_inc(s_carry, 1)
                    dve.wait_ge(s_carry, UN // 2 * q + n + 1)
                dve.tensor_tensor(dA[:, n % 2], dA[:, n % 2], c_bc[:, g, :].unsqueeze(1).to_broadcast([P, J, T]),
                                  ALU.mult).then_inc(s_hc, 1)

            def gated(q, pq, c):
                wait(dve, s_ymm, UN * q + G * (c + 1))
                wait(dve, s_uc, CC * q + c + 1)
                dve.scalar_tensor_tensor(uc[:, pq, c, :], uc[:, pq, c, :], chan_s[:, c, TAPS + 2:TAPS + 3], yps[:, c % 2, :],
                                         ALU.mult, ALU.add).then_inc(s_yd, 1)
                dve.wait_ge(s_yd, CC * q + c + 1)
                wait(dve, s_sz, q + 1)
                dve.tensor_tensor(sz[:, pq, c, :], uc[:, pq, c, :], sz[:, pq, c, :], ALU.mult).then_inc(s_yg, 1)

            def residual(q, pq):
                wait(dve, s_x2r, 16 * q)
                for a in range(2):
                    bank, number, _ = place_of(q, pq, f"O{a}")
                    wait(dve, s_ring, number)
                    dst = x2[:, 2 * a:2 * a + 2, :]
                    dve.tensor_tensor(dst, bank.rearrange("p (i d) -> p i d", d=DM), dst, ALU.add).then_inc(s_x2, 1)
                    dve.wait_ge(s_x2, 2 * (q - 1) + a + 1)
                    dve.sem_inc(s_rdve, 1)

            def norm_x2(q):
                wait(dve, s_rs2, q)
                wait(dve, s_sct, 32 * NT * (q - 1))
                for i in range(NT):
                    last = dve.tensor_scalar(xf[:, i, :], x2[:, i, :], mv[:, 1, i, 0:1], rst[:, 1, i, 1:2], ALU.subtract, ALU.mult)
                last.then_inc(s_xf, 1)

            def chain(s, base):
                done = [base]

                def then(ins):
                    ins.then_inc(s, 1)
                    done[0] = done[0] + 1
                    dve.wait_ge(s, done[0])

                return then

            def route(q, pq):
                then = chain(s_lg, LG * (q - 1))
                bank, number, _ = place_of(q, pq, "R0")
                wait(dve, s_ring, number)
                src = bank[:, 0:NT * NE].rearrange("p (i e) -> p i e", e=NE)
                then(dve.tensor_tensor(lg[:], src, rb_s[:].unsqueeze(1).to_broadcast([P, NT, NE]), ALU.add))
                dve.sem_inc(s_rdve, 1)
                for i in range(NT):
                    last = dve.max(mx[:, i, :], lg[:, i, :])
                then(last)
                dve.tensor_tensor(gap[:, :, 0], mx[:, :, 1], mx[:, :, 0], ALU.subtract).then_inc(s_gap, 1)
                for i in range(NT):
                    last = dve.max_index(ix[:, i, :], mx[:, i, :], lg[:, i, :])
                then(last)
                then(dve.tensor_copy(ixf[:], ix[:, :, 0:2]))
                for i in range(NT):
                    for k in range(2):
                        last = dve.tensor_scalar(hot[:, k, i, :], iota, ixf[:, i, k:k + 1], None, ALU.is_equal)
                then(last)
                dve.tensor_tensor(hot[:, 2], hot[:, 0], hot[:, 1], ALU.add).then_inc(s_hot, 1)
                wait(dve, s_ge, q)
                w = w12[:, 1 - pq]
                then(dve.tensor_scalar(w[:, 1, :], gap[:, :, 1], 1.0, 2.0, ALU.add, ALU.mult))
                then(dve.reciprocal(w[:, 0, :], w[:, 1, :]))
                then(dve.tensor_tensor(w[:, 1, :], w[:, 0, :], gap[:, :, 1], ALU.mult))

            def place(q, pq):
                then = chain(s_place, PL * (q - 1))
                bank, number, _ = place_of(q, pq, "K0")
                wait(dve, s_ring, number)
                then(dve.tensor_copy(r5[:], bank[:, 0:(NT + 1) * NE].rearrange("p (i e) -> p i e", e=NE)))
                dve.sem_inc(s_rdve, 1)
                then(dve.tensor_tensor(fill[:], r5[:, NT, :].unsqueeze(2).to_broadcast([P, NE, NT]),
                                       fills.unsqueeze(1).to_broadcast([P, NE, NT]), ALU.is_gt))
                then(dve.tensor_reduce(ntile[:], fill[:], AX_X, ALU.add))
                then(dve.tensor_tensor_scan(end[:], ones_e, ntile[:], 0.0, ALU.mult, ALU.add))
                then(dve.tensor_tensor(start[:], end[:], ntile[:], ALU.subtract))
                then(dve.scalar_tensor_tensor(row[:], start[:].unsqueeze(1).to_broadcast([P, NT, NE]), float(P),
                                              r5[:, 0:NT, :], ALU.mult, ALU.add))
                then(dve.tensor_tensor(row2[:], hot[:, 0:2], row[:].unsqueeze(1).to_broadcast([P, 2, NT, NE]), ALU.mult))
                dve.tensor_tensor(past[:], end[:].unsqueeze(1).to_broadcast([P, NK, NE]),
                                  iota_k.unsqueeze(2).to_broadcast([P, NK, NE]), ALU.is_le).then_inc(s_past, 1)
                then(dve.tensor_reduce(posf[:], row2[:], AX_X, ALU.add))
                dve.tensor_copy(pos[:, 1 - pq], posf[:]).then_inc(s_pos, 1)
                wait(dve, s_past, q)
                then(dve.tensor_reduce(tef[:], past[:], AX_X, ALU.add))
                dve.tensor_scalar(te[:, 1 - pq, :], tef[:], float(NE - 1), None, ALU.min).then_inc(s_te, 1)

            def activate(q, pq, k):
                v, b = NK * q + k, (pq + k) % 2
                wait(dve, s_tanh, v + 1)
                dve.scalar_tensor_tensor(th[:, b, :], th[:, b, :], 1.0, p_g[:, 0:DM], ALU.add, ALU.mult).then_inc(s_ga, 1)
                dve.wait_ge(s_ga, v + 1)
                dve.tensor_tensor(th[:, b, :], th[:, b, :], p_g[:, DM:2 * DM], ALU.mult).then_inc(s_h, 1)

            def combine(q, pq, i):
                v = NT * q + i
                wait(dve, s_xr[i % 2], 16 * (2 * q + i // 2 + 1))
                wait(dve, s_pair[i % 2], 32 * (2 * q + i // 2 + 1))
                x_i = xr[:, i % 2, :]
                dve.scalar_tensor_tensor(x_i, pair[:, i % 2, 0, :], w12[:, pq, 0, i:i + 1], x_i, ALU.mult, ALU.add).then_inc(s_mix, 1)
                dve.wait_ge(s_mix, v + 1)
                dve.scalar_tensor_tensor(x_i, pair[:, i % 2, 1, :], w12[:, pq, 1, i:i + 1], x_i, ALU.mult, ALU.add).then_inc(s_comb, 1)

            def front_slot(q, pq, n, tails):
                if n == 0:
                    wait(dve, s_x, 16 * (q + 1))
                    moments(0, xin, s_mv, q + tails + 1)
                if n == 2:
                    norm_x(q, pq)
                if n in (4, 5, 6, 7):
                    conv(q, pq, n - 4)
                if n in DT_SLOTS:
                    softplus(q, pq, DT_SLOTS.index(n))

            def step(q, pq, front, tail, old, scan):
                for n in range(UN):
                    if scan:
                        unit(q, pq, n)
                    if tail:
                        if n == 2:
                            residual(q, pq)
                            moments(1, x2, s_mv2, (2 * q + 2 if front else NQ + q))
                        if n == 4:
                            norm_x2(q)
                        if n == 5:
                            route(q, pq)
                        if n == 6:
                            place(q, pq)
                    if scan:
                        weigh(q, pq, n)
                        if n % G == 0 and n:
                            gated(q, pq, n // G - 1)
                    if tail and n == 0:
                        gated(q - 1, 1 - pq, CC - 1)
                    if front:
                        front_slot(q + 1, 1 - pq, n, q - 1 if tail else 0)
                    if old and n in (12, 14):
                        for i in ((0, 1) if n == 12 else (2, 3)):
                            combine(q - 2, pq, i)
                    for c, pc, at in positions(q, pq, n, tail, old):
                        if 0 <= at - 1 < NK:
                            activate(c, pc, at - 1)

            for n in range(UN):
                front_slot(0, 0, n, 0)
            steps(dve, step)

        @block.gpsimd
        def _(pool):
            pool.memset(xd[:], 0.0).then_inc(s_init, 1)
            pool.memset(nhalf[:], -0.5).then_inc(s_init, 1)
            pool.memset(eps[:], EPS).then_inc(s_init, 1)
            pool.memset(xf[:, 0, :], 0.0).then_inc(s_init, 1)
            pool.wait_ge(s_init, 4)

            def deviation(k, q, mvs, done):
                wait(pool, mvs, q + 1)
                base = (2 * q if k == 0 else 0)
                s = s_pow if k == 0 else s_pow2
                n = 5 if k == 0 else 1
                pool.tensor_tensor(rst[:, k, :, 0], mv[:, k, :, 1], eps[:], ALU.add).then_inc(s, 1)
                pool.wait_ge(s, n * q + 1)
                ins = pool.tensor_tensor(rst[:, k, :, 1], rst[:, k, :, 0], nhalf[:], ALU.pow)
                if k == 1:
                    ins.then_inc(done, 1)
                    return
                ins.then_inc(s, 1)
                pool.wait_ge(s, n * q + 2)
                pool.tensor_tensor(rst[:, k, :, 2], rst[:, k, :, 1], rst[:, k, :, 1], ALU.mult).then_inc(s, 1)
                pool.wait_ge(s, n * q + 3)
                pool.tensor_tensor(rst[:, k, :, 2], rst[:, k, :, 2], mv[:, k, :, 1], ALU.mult).then_inc(s, 1)
                pool.wait_ge(s, n * q + 4)
                pool.tensor_tensor(rst[:, k, :, 2], rst[:, k, :, 2], eps[:], ALU.add).then_inc(s, 1)
                pool.wait_ge(s, n * q + 5)
                pool.tensor_tensor(rst[:, k, :, 3], rst[:, k, :, 2], nhalf[:], ALU.pow).then_inc(done, 1)

            def softplus(q, pq, c):
                v = CC * q + c
                wait(pool, s_m, v + 1)
                pool.tensor_tensor(t_r[:], t_e[:], t_r[:], ALU.subtract).then_inc(s_sp, 1)
                wait(pool, s_l, v + 1)
                pool.wait_ge(s_sp, 3 * v + 1)
                pool.tensor_tensor(t_r[:], t_r[:], dtb[:, c % 2, :], ALU.add).then_inc(s_sp, 1)
                pool.wait_ge(s_sp, 3 * v + 2)
                pool.tensor_tensor(dtb[:, c % 2, :], t_r[:], t_m[:], ALU.add).then_inc(s_sp, 1)
                pool.wait_ge(s_sp, 3 * v + 3)
                wait(pool, s_uc, v + 1)
                pool.tensor_tensor(dtub[:, c % 2, :], dtb[:, c % 2, :], uc[:, pq, c, :], ALU.mult).then_inc(s_dt, 1)

            def unit(q, n):
                c, g = n // G, n % G
                if g == 0:
                    wait(pool, s_rdtu[c % 2], 64 * (2 * q + c // 2 + 1))
                if c == 0:
                    wait(pool, s_bc[g], 128 * (q + 1))
                wait(pool, s_scan, UN * q + n - 1)
                pool.tensor_tensor(dBu[:, n % 2], rep_dtu[:, c % 2], b_bc[:, g, :].unsqueeze(1).to_broadcast([P, J, T]),
                                   ALU.mult).then_inc(s_dbu, 1)

            def scatter(q, pq, i):
                wait(pool, s_pos, q + 1)
                pool.sem_inc(s_free, 1)
                for k in range(2):
                    pool.indirect_dma_start(out=sorted_x[pq], out_offset=bass.IndirectOffsetOnAxis(ap=pos[:, pq, k, i:i + 1], axis=0),
                                            in_=xf[:, i, :], in_offset=None).then_inc(s_sct, 16)

            def gather(q, pq, i):
                for k in (NK - 2, NK - 1):
                    wait(pool, s_ys[(pq + k) % 2], tiles_even(q, pq, k))
                wait(pool, s_comb, NT * q + i - 1)
                pool.sem_inc(s_free, 1)
                for k in range(2):
                    pool.indirect_dma_start(out=pair[:, i % 2, k, :], out_offset=None, in_=sorted_y[pq],
                                            in_offset=bass.IndirectOffsetOnAxis(ap=pos[:, pq, k, i:i + 1], axis=0)).then_inc(s_pair[i % 2], 16)

            def step(q, pq, front, tail, old, scan):
                for n in range(UN):
                    if scan and n + 1 < UN:
                        unit(q, n + 1)
                    if front and n + 1 == UN:
                        unit(q + 1, 0)
                    if tail:
                        if n == 3:
                            deviation(1, q - 1, s_mv2, s_rs2)
                        if n in (6, 7):
                            for i in ((0, 1) if n == 6 else (2, 3)):
                                scatter(q - 1, 1 - pq, i)
                    if old and n in (11, 13):
                        for i in ((0, 1) if n == 11 else (2, 3)):
                            gather(q - 2, pq, i)
                    if front:
                        if n == 1:
                            deviation(0, q + 1, s_mv, s_rs)
                        if n in DT_SLOTS:
                            softplus(q + 1, 1 - pq, DT_SLOTS.index(n))

            pool.wait_ge(s_zero, 32)
            deviation(0, 0, s_mv, s_rs)
            for c in range(CC):
                softplus(0, 0, c)
            unit(0, 0)
            steps(pool, step)


def program(nc, args):
    mamba_moe(nc, *args)


def kernel(**inputs):
    import concourse.bacc as bacc
    from concourse.bass_utils import run_bass_kernel_spmd

    i = {k[3:]: np.asarray(v) for k, v in inputs.items()}

    def rows(a, k):
        return a.reshape(k, P, -1).transpose(1, 0, 2)

    def cols(a, k):
        return a.reshape(k, P).T

    w_dt = np.zeros((P, DI), np.float32)
    w_dt[:RANK] = i["attn_W_dt"].T
    chan = np.concatenate([rows(i["attn_conv_w"], CC)] + [cols(i[n], CC)[:, :, None] for n in
                          ("attn_conv_b", "attn_b_dt", "attn_D")], axis=2)
    a_log = i["attn_A_log"].reshape(CC, J, 32, G, R).transpose(4, 2, 0, 3, 1).reshape(P, UN, J)
    moe = np.concatenate(
        [np.concatenate([i["ffn_we_gate"], i["ffn_we_up"]], axis=2).reshape(NE, DC, P, 2 * DM).transpose(0, 2, 1, 3).reshape(NE, P, -1),
         i["ffn_we_down"].reshape(NE, DC, P, DM).transpose(0, 2, 1, 3).reshape(NE, P, -1)], axis=2)
    lane = np.arange(P)
    consts = np.concatenate([np.eye(P), lane[:, None] % 32 == np.arange(32)[None, :],
                             lane[:, None] < lane[None, :], np.ones((P, P)), np.tile(np.arange(NE), (P, 1)),
                             np.ones((P, NE)), np.tile(P * np.arange(NT), (P, 1)), np.tile(np.arange(NK), (P, 1))],
                            axis=1).astype(np.float32)
    arrays = {
        "x": i["attn_x"],
        "w_in": rows(i["attn_W_in"].T, DC),
        "w_xp": rows(i["attn_W_xp"].T, CC),
        "w_dt": w_dt,
        "w_out": rows(i["attn_W_out"].T, CC),
        "w_moe": moe,
        "chan": chan,
        "a_log": a_log,
        "ln_gb": np.stack([cols(i["attn_ln_g"], DC), cols(i["attn_ln_b"], DC)], axis=1),
        "r_w": rows(i["ffn_router_w"], DC),
        "r_b": np.broadcast_to(i["ffn_router_b"], (P, NE)),
        "consts": consts,
    }
    arrays = {k: np.ascontiguousarray(v) for k, v in arrays.items()}
    nc = bacc.Bacc("TRN2", target_bir_lowering=False, num_devices=1)
    args = [nc.dram_tensor(f"in_{k}", a.shape, mybir.dt.from_np(a.dtype), kind="ExternalInput").ap()
            for k, a in arrays.items()]
    args.append(nc.dram_tensor("out_0", (BATCH, SEQ, DM), F32, kind="ExternalOutput").ap())
    order = ["x", "w_in", "w_xp", "w_dt", "w_out", "w_moe", "chan", "a_log", "ln_gb", "r_w", "r_b", "consts"]
    assert list(arrays) == order
    program(nc, args)
    r = run_bass_kernel_spmd(nc, [{f"in_{k}": a for k, a in arrays.items()}], core_ids=[0])
    return r.results[0]["out_0"]
```
